# Optimizing a Trainium2 kernel written in Bass

```python
import numpy as np
import jax
import jax.numpy as jnp

def _softmax(x, axis=-1):
    return jax.nn.softmax(x, axis=axis)

def _gelu(x):
    return jax.nn.gelu(x, approximate=True)

def _silu(x):
    return jax.nn.silu(x)

def _sigmoid(x):
    return jax.nn.sigmoid(x)

def _layernorm(x, axis=-1, eps=1e-05):
    m = jnp.mean(x, axis=axis, keepdims=True)
    v = jnp.var(x, axis=axis, keepdims=True)
    return (x - m) / jnp.sqrt(v + eps)

def _scatter_add(tgt, idx, src, axis=0):
    return tgt.at[idx].add(src)

def _segment_sum(src, seg, n):
    return jax.ops.segment_sum(src, seg, n)
kernel_name = 'mk_seq_postln_d1_jaxref_r8_1719be'

def setup_inputs(seed: int=0):
    np.random.seed(seed)
    _w = jnp.asarray

    def _L0_attn_setup():
        import jax, jax.numpy as jnp
        import numpy as np
        import math
        N_HEADS = 16
        WINDOW_SIZE = 128
        DILATION = 4

        def _sparse_mask(S, window, dilation):
            i = jnp.arange(S)[:, None]
            j = jnp.arange(S)[None, :]
            win = (j <= i) & (j >= i - window + 1)
            base = i - window - dilation
            dil = (j <= base) & (jnp.mod(base - j, dilation) == 0)
            return win | dil
        key = jax.random.key(seed)
        k1, k2, k3 = jax.random.split(key, 3)
        B, S, D = (2, 256, 128)
        x = jax.random.normal(k1, (B, S, D), dtype=jnp.float32)
        qkv = 0.01 * jax.random.normal(k2, (3 * D, D), dtype=jnp.float32)
        wo = 0.01 * jax.random.normal(k3, (D, D), dtype=jnp.float32)
        return {'x': x, 'qkv': qkv, 'wo': wo}
    _L0_attn_in = _L0_attn_setup()

    def _L0_ffn_setup():
        import jax, jax.numpy as jnp
        import numpy as np
        NUM_EXPERTS = 8
        TOP_K = 2
        D = 128
        H = 4 * D
        B, S = (4, 256)
        key = jax.random.key(seed)
        ks = jax.random.split(key, 8)
        s = 0.02
        return {'x': jax.random.normal(ks[0], (B, S, D), dtype=jnp.float32), 'gate_w': jax.random.normal(ks[1], (NUM_EXPERTS, D), dtype=jnp.float32) * s, 'gate_b': jnp.zeros((NUM_EXPERTS,), dtype=jnp.float32), 'w1': jax.random.normal(ks[2], (NUM_EXPERTS, D, H), dtype=jnp.float32) * s, 'b1': jnp.zeros((NUM_EXPERTS, H), dtype=jnp.float32), 'w2': jax.random.normal(ks[3], (NUM_EXPERTS, H, D), dtype=jnp.float32) * s, 'b2': jnp.zeros((NUM_EXPERTS, D), dtype=jnp.float32)}
    _L0_ffn_in = _L0_ffn_setup()
    _d = {'L0_attn_x': _L0_attn_in['x'], 'L0_attn_qkv': _L0_attn_in['qkv'], 'L0_attn_wo': _L0_attn_in['wo'], 'L0_ffn_gate_w': _L0_ffn_in['gate_w'], 'L0_ffn_gate_b': _L0_ffn_in['gate_b'], 'L0_ffn_w1': _L0_ffn_in['w1'], 'L0_ffn_b1': _L0_ffn_in['b1'], 'L0_ffn_w2': _L0_ffn_in['w2'], 'L0_ffn_b2': _L0_ffn_in['b2']}
    _x0 = _d['L0_attn_x']
    _d['L0_attn_x'] = jax.random.normal(jax.random.fold_in(jax.random.key(seed), 1), (8, 512, 128), dtype=_x0.dtype)
    del _x0
    return _d

def reference(L0_attn_x, L0_attn_qkv, L0_attn_wo, L0_ffn_gate_w, L0_ffn_gate_b, L0_ffn_w1, L0_ffn_b1, L0_ffn_w2, L0_ffn_b2):

    def _L0_attn_ref(x, qkv, wo):
        import jax, jax.numpy as jnp
        import numpy as np
        import math
        N_HEADS = 16
        WINDOW_SIZE = 128
        DILATION = 4

        def _sparse_mask(S, window, dilation):
            i = jnp.arange(S)[:, None]
            j = jnp.arange(S)[None, :]
            win = (j <= i) & (j >= i - window + 1)
            base = i - window - dilation
            dil = (j <= base) & (jnp.mod(base - j, dilation) == 0)
            return win | dil
        B, S, D = x.shape
        H = N_HEADS
        dh = D // H
        QKV = x @ qkv.T
        Q, K, V = jnp.split(QKV, 3, axis=-1)
        q = Q.reshape(B, S, H, dh)
        k = K.reshape(B, S, H, dh)
        v = V.reshape(B, S, H, dh)
        scores = jnp.einsum('bihd,bjhd->bhij', q, k) / math.sqrt(float(dh))
        mask = _sparse_mask(S, WINDOW_SIZE, DILATION)
        scores = jnp.where(mask[None, None, :, :], scores, jnp.float32(-jnp.inf))
        attn = jax.nn.softmax(scores, axis=-1)
        out = jnp.einsum('bhij,bjhd->bihd', attn, v).reshape(B, S, D)
        return out @ wo.T

    def _L0_ffn_ref(x, gate_w, gate_b, w1, b1, w2, b2):
        import jax, jax.numpy as jnp
        import numpy as np
        NUM_EXPERTS = 8
        TOP_K = 2
        D = 128
        H = 4 * D
        B, S = (4, 256)
        orig_shape = x.shape
        xf = x.reshape(-1, orig_shape[-1])
        gates = xf @ gate_w.T + gate_b
        weights, indices = jax.lax.top_k(gates, TOP_K)
        weights = jax.nn.softmax(weights, axis=-1)
        out = jnp.zeros_like(xf)
        for e in range(NUM_EXPERTS):
            w_e = jnp.sum(weights * (indices == e), axis=-1, keepdims=True)
            h = jax.nn.gelu(xf @ w1[e] + b1[e], approximate=False)
            out = out + w_e * (h @ w2[e] + b2[e])
        return out.reshape(orig_shape)
    x = L0_attn_x
    x = _layernorm(x + _L0_attn_ref(x, L0_attn_qkv, L0_attn_wo), axis=-1)
    x = _layernorm(x + _L0_ffn_ref(x, L0_ffn_gate_w, L0_ffn_gate_b, L0_ffn_w1, L0_ffn_b1, L0_ffn_w2, L0_ffn_b2), axis=-1)
    return x

_drawn_inputs = setup_inputs


def setup_inputs(seed=0):
    import zlib

    import numpy as np

    out = dict(_drawn_inputs(seed))
    spreads = {'L0_ffn_gate_b': (0.0, 0.1), 'L0_ffn_b1': (0.0, 0.485), 'L0_ffn_b2': (0.0, 0.1)}
    factors = {'L0_attn_qkv': 8.0, 'L0_attn_wo': 8.0}
    for name, (base, spread) in spreads.items():
        noise = np.random.default_rng([zlib.crc32(name.encode()), seed]).standard_normal(out[name].shape)
        drawn = base * np.exp(spread * noise) if base else spread * noise
        out[name] = jnp.asarray(drawn.astype(out[name].dtype))
    for name, factor in factors.items():
        out[name] = (out[name] * factor).astype(out[name].dtype)
    return out
```

```python
from contextlib import ExitStack

import concourse.bass as bass
from concourse import mybir

FP32 = mybir.dt.float32
FP32R = mybir.dt.float32r
BF16 = mybir.dt.bfloat16
ALU = mybir.AluOpType
ACT = mybir.ActivationFunctionType
AX = mybir.AxisListType

B, S, D = 8, 512, 128
H, DH = 16, 8
P = 128
NB = S // P
WINDOW, DILATION = 128, 4
E, FH = 8, 512
NCH = FH // P
CH = E * NCH
EPS = 1e-5
SCALE = float(DH) ** -0.5
MASKED = -1e30
BELOW = -3e38

G = 4
UNITS = 4
SLOTS = G * UNITS
ROW_M = 24
VW = DH + 1
OFF = [0, 512, 896, 1152]
PW = 1280
KEY_CHUNKS = [[(0, 0)], [(1, 0)], [(2, 0), (3, 256)]]
CHUNK_AT = [0, 512, 896, 1280]
QUERY_CHUNKS = [[(3, 0)], [(2, 0), (0, 384)], [(1, 0)]]
NC3 = 3

PREP = [(0, "xT"), (2, "q"), (3, "k"), (4, "V")]
POST = [(6, "OA"), (7, "OB"), (8, "AT"), (10, "proj"), (11, "yT"), (12, "gate")]
MAXES = [(1, "m1"), (5, "m2"), (9, "m3"), (13, "m0")]
BODY_FIRST = sorted(PREP + MAXES)
BODY_MID = sorted(PREP + MAXES + POST)
BODY_LAST = sorted(MAXES[:3] + POST)
START = ["w0", "w1", "w2", "w3", "gw", "b1", "xT", "q", "k", "V", "m0"]
BASE_MID = len(START) + len(BODY_FIRST)
BASE_LAST = BASE_MID + len(BODY_MID) * (B - 2)
BASE_TAIL = BASE_LAST + len(BODY_LAST)


def is_at(b, n):
    return isinstance(b, int) and b == n


def body_steps(b):
    return BODY_FIRST if is_at(b, 0) else BODY_LAST if is_at(b, B - 1) else BODY_MID


def in_body(b, name):
    k = [n for _, n in body_steps(b)].index(name) + 1
    if is_at(b, 0):
        return len(START) + k
    if is_at(b, B - 1):
        return BASE_LAST + k
    return BASE_MID + len(BODY_MID) * (b - 1) + k


def side_of(name, b):
    if name in ("xT", "q", "k", "V", "m0"):
        return START.index(name) + 1 if is_at(b, 0) else in_body(b - 1, name)
    if name in ("m1", "m2", "m3"):
        return in_body(b, name)
    if is_at(b, B - 1):
        return BASE_TAIL + [n for _, n in POST].index(name) + 1
    return in_body(b + 1, name)


FF_POST = [(10, "out")]
FF_PREP = [(16, "wT"), (20, "b2")]
LAG = 2


def ff_side_of(name, f):
    if name == "out":
        return 3 * B if is_at(f, B - 1) else 2 + 2 + 3 * f + 1
    k = 1 if name == "wT" else 2
    if is_at(f, 0):
        return k
    if is_at(f, 1):
        return 2 + k
    return 2 + 2 + 3 * (f - 2) + 1 + k


def build(nc, x, qkv, wo, gate_w, gate_b, w1, b1, w2, b2, maskq, maskk, ident, select, out):
    ctx = ExitStack()
    with ctx:
        def sb(name, shape, dt=FP32):
            return ctx.enter_context(nc.sbuf_tensor(name, shape, dt))

        def pb(name):
            return ctx.enter_context(nc.psum_tensor(name, [P, S], FP32))

        def sem(name):
            return ctx.enter_context(nc.semaphore(name))

        QS = sb("QS", [P, 2, H, S], FP32R)
        KS = sb("KS", [P, 2, UNITS, S], FP32R)
        split = sb("split", [P, 4, S], FP32R)
        PR = sb("PR", [P, 2, G, PW])
        VA = sb("VA", [P, 2, NB, H, 2 * VW])
        yT_all = sb("yT_all", [P, B, S])
        w_all = sb("w_all", [P, B, NB, 2, E])
        W1 = sb("W1", [P, E, FH])
        x_in = sb("x_in", [P, NB, D])
        y = sb("y", [P, NB, D])
        T = sb("T", [P, S])
        O_sb = sb("O_sb", [P, 2, S])
        att = sb("att", [P, NB, D])
        mask_q = sb("mask_q", [P, S], BF16)
        mask_k = sb("mask_k", [P, S], BF16)
        idf = sb("idf", [P, P])
        idb = sb("idb", [P, P], BF16)
        sel = sb("sel", [2 * E, E, P], FP32R)
        wrows = W1[:, 4, :].rearrange("p (i d) -> p i d", i=4)
        grows = W1[:, 6, 0:P]
        select_in = W1[0:2 * E, 0:2, :].rearrange("j a c -> j (a c)")
        one_row = W1[0:1, 5, :]
        WT = sb("WT", [P, 4, D])
        gwT = sb("gwT", [P, E])
        b1T = sb("b1T", [P, CH])
        b2s = sb("b2s", [2 * E, D])
        gbias = sb("gbias", [P, E])
        rank = sb("rank", [P, E])
        mx = sb("mx", [P, 2, NB, G])
        zero_row = sb("zero_row", [1, S])
        rec = sb("rec", [P, 2, NB, G, 2])
        stats = sb("stats", [P, NB, 6])
        mean_var = sb("mean_var", [P, NB, 2])
        var_eps = sb("var_eps", [P, NB])
        rstd = sb("rstd", [P, NB])
        minus_half = sb("minus_half", [P, NB])
        gt = sb("gt", [P, 6, NB, E])
        gs = sb("gs", [P, 8, NB])
        w_hl = sb("w_hl", [P, NB, 2, E], FP32R)
        w_tok = sb("w_tok", [P, NB, 2, E])
        wT = sb("wT", [2 * E, 2, S], FP32R)
        m_row = wT[0:G, :, :]

        ST = [pb(f"ST{i}") for i in range(3)]
        SM = [pb(f"SM{i}") for i in range(2)]
        OP = [pb(f"OP{i}") for i in range(2)]
        SIDE = pb("SIDE")
        HB = ST + [OP[1]]
        OE = SM
        WB = OP[0]

        scratch = nc.dram_tensor("scratch", [2, 2, P, S], FP32, kind="Internal").ap()

        const_in, mask_in, ones_in, w1_in = sem("const_in"), sem("mask_in"), sem("ones_in"), sem("w1_in")
        x_loaded, xres_loaded = sem("x_loaded"), sem("xres_loaded")
        w2_in = [sem(f"w2_in{e}") for e in range(E)]
        cleared_dve, cleared_pool, idb_ready = sem("cleared_dve"), sem("cleared_pool"), sem("idb_ready")
        side_filled, side_drained = sem("side_filled"), sem("side_drained")
        hi_ready, scratch_in, stack_in, mrow_in = sem("hi_ready"), sem("scratch_in"), sem("stack_in"), sem("mrow_in")
        smax_filled, smax_read = sem("smax_filled"), sem("smax_read")
        st_filled, exp_done, pv_done, o_copied = sem("st_filled"), sem("exp_done"), sem("pv_done"), sem("o_copied")
        norm_step, ln_step, y_ready = sem("norm_step"), sem("ln_step"), sem("y_ready")
        gate_step, gexp_ready, w_ready, kept = sem("gate_step"), sem("gexp_ready"), sem("w_ready"), sem("kept")
        w1_split, w2_split, y_split = sem("w1_split"), sem("w2_split"), sem("y_split")
        h_filled, gelu_done, hhi_done, hlo_done = sem("h_filled"), sem("gelu_done"), sem("hhi_done"), sem("hlo_done")
        w2_done, wb_filled, wb_copied = sem("w2_done"), sem("wb_filled"), sem("wb_copied")
        scaled, added, ff_filled, ff_drained = sem("scaled"), sem("added"), sem("ff_filled"), sem("ff_drained")
        wtok_ready, ff_step, out_in = sem("wtok_ready"), sem("ff_step"), sem("out_in")
        sel_in, sel_ready = sem("sel_in"), sem("sel_ready")
        past_wait = sem("past_wait")
        var_ready, rstd_ready = sem("var_ready"), sem("rstd_ready")

        prf = PR[:, :, :, :].rearrange("p a g c -> p (a g c)")
        hf = [prf[:, S * i:S * (i + 1)] for i in range(4)]
        wb_sb = [prf[:, S * (4 + i):S * (5 + i)] for i in range(2)]
        part = [prf[:, S * (6 + i):S * (7 + i)] for i in range(2)]
        acc = [prf[:, S * (8 + i):S * (9 + i)] for i in range(2)]
        out_sb = [prf[:, S * (10 + i):S * (11 + i)] for i in range(2)]
        W2 = [prf[:, S * (12 + e):S * (13 + e)].rearrange("p (c d) -> p c d", c=NCH) for e in range(E)]

        block = ctx.enter_context(nc.Block())

        x_v = x.rearrange("b (k p) d -> b p k d", p=P)
        out_v = out.rearrange("b (k p) d -> b p k d", p=P)
        STACK_IN = 16 * (G + 2 * 3 * G)
        SCRATCH_IN = 16 * 4

        def at_batch(v, b):
            return v[b] if isinstance(b, int) else v[bass.ds(b, 1)].rearrange("o p k d -> (o p) k d")

        def batches(eng, body):
            body(0, 0)
            with eng.Fori(0, (B - 2) // 2) as i:
                body(i * 2 + 1, 1)
                body(i * 2 + 2, 0)
            body(B - 1, 1)

        def own_wait(eng):
            eng.sem_inc(past_wait, 1)

        def unit_of(b, p, s):
            return (b, p, s) if s < UNITS else (b + 1, 1 - p, s - UNITS)

        @block.sync
        def _(sp):
            sp.dma_start(idf[:], ident[:, :]).then_inc(const_in, 16)
            for i in range(3):
                sp.dma_start(wrows[:, i, :], qkv[i * D:(i + 1) * D, :]).then_inc(const_in, 16)
            sp.dma_start(wrows[:, 3, :], wo[:, :]).then_inc(const_in, 16)
            sp.dma_start(grows[0:E, :], gate_w[:, :]).then_inc(const_in, 16)
            sp.dma_start(grows[32:64, :], b1.rearrange("e (c p) -> (e c) p", p=P)).then_inc(const_in, 16)
            sp.dma_start(x_in[:], x_v[0]).then_inc(x_loaded, 16)
            sp.dma_start(mask_q[:], maskq[:, :]).then_inc(mask_in, 16)
            sp.dma_start(mask_k[:], maskk[:, :]).then_inc(mask_in, 16)
            sp.dma_start(b2s[0:E, :], b2[:, :]).then_inc(mask_in, 16)
            sp.dma_start(b2s[E:2 * E, :], b2[:, :]).then_inc(mask_in, 16)
            sp.dma_start(gbias[:], gate_b.rearrange("(o e) -> o e", o=1).broadcast_to([P, E])).then_inc(mask_in, 16)
            sp.dma_start(select_in, select[:, :]).then_inc(sel_in, 16)
            sp.dma_start(y[:], x_v[0]).then_inc(xres_loaded, 16)

            def m_rows(b, p, s):
                sp.wait_ge(side_drained, side_of(f"m{s}", b))
                for g in range(G):
                    sp.dma_start(QS[32 * g + ROW_M:32 * g + ROW_M + 1, p, G * g + s, :].bitcast(FP32),
                                 m_row[g:g + 1, s % 2, :].bitcast(FP32)).then_inc(mrow_in, 16)

            def stacks(b, p):
                for j, name in enumerate("qk"):
                    sp.wait_ge(side_drained, side_of(name, b))
                    for t in range(2):
                        sp.dma_start(scratch[j, t], split[:, 2 * j + t, :].bitcast(FP32)).then_inc(scratch_in, 16)
                for g in range(G):
                    sp.dma_start(QS[32 * g + ROW_M:32 * g + ROW_M + 1, p, 4 * g:4 * g + 4, :].bitcast(FP32),
                                 zero_row[:, :].unsqueeze(1).broadcast_to([1, 4, S])).then_inc(stack_in, 16)
                sp.wait_ge(scratch_in, (b + 1) * SCRATCH_IN)
                for j in range(2):
                    for g in range(G):
                        for t, part_ in enumerate([(0, 0, 1), (0, 1, 0)][j]):
                            r = 32 * g + DH * t
                            dst = KS[r:r + DH, p, :, :] if j else QS[r:r + DH, p, 4 * g:4 * g + 4, :]
                            src = scratch[j, part_, 32 * g:32 * g + 32, :].rearrange("(s d) c -> d s c", d=DH)
                            sp.dma_start(dst.bitcast(FP32), src).then_inc(stack_in, 16)

            sp.wait_ge(cleared_dve, 1)
            stacks(0, 0)
            sp.wait_ge(cleared_pool, 1)
            for p in range(2):
                for g in range(G):
                    r = 32 * g + ROW_M
                    sp.dma_start(KS[r:r + 1, p, :, :].bitcast(FP32),
                                 one_row.unsqueeze(1).broadcast_to([1, UNITS, S])).then_inc(ones_in, 16)
            sp.wait_ge(side_filled, side_of("xT", 0))
            sp.dma_start(x_in[:], x_v[1]).then_inc(x_loaded, 16)
            m_rows(0, 0, 0)
            sp.wait_ge(sel_ready, 1)
            sp.wait_ge(ones_in, 16 * 2 * G)
            sp.dma_start(W1[:], w1.rearrange("e d f -> d e f")).then_inc(w1_in, 16)

            def body(b, p):
                m_rows(b, p, 1)
                if not is_at(b, B - 1):
                    if not is_at(b, 0):
                        sp.wait_ge(st_filled, b * (SLOTS * NC3))
                        own_wait(nc.sync)
                        sp.wait_ge(stack_in, (b + 1) * STACK_IN)
                        own_wait(nc.sync)
                    else:
                        sp.wait_ge(stack_in, STACK_IN)
                    stacks(b + 1, 1 - p)
                m_rows(b, p, 2)
                m_rows(b, p, 3)
                if not is_at(b, 0):
                    sp.wait_ge(side_filled, side_of("yT", b - 1))
                    sp.dma_start(y[:], at_batch(x_v, b)).then_inc(xres_loaded, 16)
                if not is_at(b, B - 1):
                    sp.wait_ge(side_filled, side_of("xT", b + 1))
                    own_wait(nc.sync)
                    sp.dma_start(x_in[:], at_batch(x_v, (b + 2) % B)).then_inc(x_loaded, 16)
                    m_rows(b + 1, 1 - p, 0)

            batches(sp, body)
            sp.wait_ge(pv_done, B * UNITS)
            for e in range(E):
                sp.dma_start(W2[e], w2[e].rearrange("(c p) d -> p c d", p=P)).then_inc(w2_in[e], 16)

            def store(f, p):
                sp.wait_ge(ff_drained, ff_side_of("out", f))
                sp.dma_start(at_batch(out_v, f), out_sb[p].rearrange("p (k d) -> p k d", k=NB)).then_inc(out_in, 16)

            batches(sp, store)
            sp.wait_ge(out_in, 16 * (B + 1))
            sp.wait_ge(x_loaded, 16 * (B + 1))
            sp.wait_ge(scratch_in, B * SCRATCH_IN)

        @block.gpsimd
        def _(pool):
            nc.gpsimd.sem_inc(kept, 1)
            nc.gpsimd.sem_inc(out_in, 16)
            nc.gpsimd.memset(KS[:, 1].bitcast(FP32), 0.0)
            nc.gpsimd.memset(VA[:], 0.0)
            nc.gpsimd.memset(minus_half[:], -0.5)
            nc.gpsimd.memset(QS[:, 1].bitcast(FP32), 0.0).then_inc(cleared_pool, 1)

            pool.wait_ge(sel_in, 16)
            nc.gpsimd.tensor_copy(sel[:].rearrange("j e p -> j (e p)"), select_in).then_inc(sel_ready, 1)

            def body(b, p):
                if is_at(b, 0):
                    return
                keep(b - 1)

            def power(count):
                pool.wait_ge(var_ready, count + 1)
                nc.gpsimd.tensor_tensor(rstd[:], var_eps[:], minus_half[:], ALU.pow).then_inc(rstd_ready, 1)

            def keep(f):
                power(f)
                pool.wait_ge(side_drained, side_of("yT", f))
                nc.gpsimd.tensor_copy(yT_all[:, bass.ds(f, 1), :].rearrange("p o c -> p (o c)"), T[:, :]).then_inc(kept, 1)
                pool.wait_ge(w_ready, f + 1)
                nc.gpsimd.tensor_copy(w_all[:, bass.ds(f, 1)].rearrange("p o k t e -> p (o k t e)"),
                                      w_hl[:].bitcast(FP32).rearrange("p k t e -> p (k t e)")).then_inc(kept, 1)

            batches(pool, body)
            keep(B - 1)

            def add(f, p, e):
                pool.wait_ge(scaled, f * E + e + 1)
                if e == 0:
                    pool.wait_ge(ff_drained, ff_side_of("b2", f))
                else:
                    pool.wait_ge(added, f * E + e)
                nc.gpsimd.tensor_tensor(acc[p], acc[p], part[e % 2], ALU.add).then_inc(added, 1)

            def ff_body(f, p):
                for e in range(E):
                    add(f, p, e)
                    if e == 1 and not is_at(f, 0):
                        power(f - 1 + B)

            batches(pool, ff_body)
            power(B - 1 + B)

        @block.scalar
        def _(act):
            def copy_side(dst, src, name, b, scale=None):
                act.wait_ge(side_filled, side_of(name, b))
                if scale is None:
                    return nc.scalar.copy(dst, src)
                return nc.scalar.mul(dst, src, scale)

            def evacuate(name, b, p):
                if name == "xT":
                    if not (is_at(b, 0) or is_at(b, 1)):
                        act.wait_ge(kept, (b - 2) * 2 + 1)
                    copy_side(T[:], SIDE[:], name, b).then_inc(side_drained, 1)
                elif name in "qk":
                    if not is_at(b, 0):
                        act.wait_ge(scratch_in, b * SCRATCH_IN)
                    copy_side(split[:, 2 * "qk".index(name), :], SIDE[:], name, b).then_inc(hi_ready, 1)
                elif name == "V":
                    if is_at(b, 0):
                        act.wait_ge(cleared_pool, 1)
                        act.wait_ge(cleared_dve, 1)
                    elif not is_at(b, 1):
                        act.wait_ge(pv_done, (b - 1) * UNITS)
                    src = SIDE[:].rearrange("p (k h t d) -> p k h t d", k=NB, t=2, d=DH)
                    for t in range(2):
                        last = copy_side(VA[:, p, :, t::2, VW * t:VW * t + DH], src[:, :, :, t, :], name, b)
                    last.then_inc(side_drained, 1)
                elif name[0] == "m":
                    s = int(name[1])
                    u = b * UNITS + s
                    if not (isinstance(u, int) and u < 2):
                        act.wait_ge(mrow_in, (u - 1) * (16 * G))
                    copy_side(m_row[:, s % 2, :], SIDE[0:G, :], name, b, -1.0).then_inc(side_drained, 1)
                elif name == "AT":
                    if not is_at(b, 0):
                        act.wait_ge(kept, b * 2 + 1)
                    copy_side(T[:], SIDE[:], name, b).then_inc(side_drained, 1)
                elif name == "yT":
                    copy_side(T[:], SIDE[:], name, b).then_inc(side_drained, 1)
                elif name == "gate":
                    act.wait_ge(gate_step, b * GATE_STEPS + GATE_EXP)
                    nc.scalar.activation(gs[:, 5, :], gs[:, 4, :], ACT.Exp).then_inc(gexp_ready, 1)

            def copy_o(b, half):
                act.wait_ge(pv_done, b * UNITS + 2 * half + 2)
                if not is_at(b, 0):
                    act.wait_ge(side_filled, side_of("OA" if half == 0 else "OB", b - 1))
                nc.scalar.copy(O_sb[:, half, :], OP[half][:]).then_inc(o_copied, 1)

            for i in range(4):
                act.wait_ge(side_filled, i + 1)
                nc.scalar.copy(WT[:, i, :], SIDE[:, 0:D]).then_inc(side_drained, 1)
            act.wait_ge(side_filled, 5)
            nc.scalar.copy(gwT[:], SIDE[:, 0:E]).then_inc(side_drained, 1)
            act.wait_ge(side_filled, 6)
            nc.scalar.copy(b1T[:], SIDE[:, 0:CH]).then_inc(side_drained, 1)
            for name in START[6:]:
                evacuate(name, 0, 0)

            def body(b, p):
                for i in range(SLOTS):
                    s, g = divmod(i, G)
                    u = b * UNITS + s
                    if g == 0 and not (isinstance(u, int) and u < 2):
                        act.wait_ge(pv_done, u - 1)
                    for c in range(NC3):
                        act.wait_ge(st_filled, b * (SLOTS * NC3) + i * NC3 + c + 1)
                        n = CHUNK_AT[c + 1] - CHUNK_AT[c]
                        nc.scalar.activation(PR[:, s % 2, g, CHUNK_AT[c]:CHUNK_AT[c + 1]], ST[c][:, 0:n],
                                             ACT.Exp, scale=SCALE).then_inc(exp_done, 1)
                    if i == 5 and not is_at(b, 0):
                        copy_o(b - 1, 1)
                    if i == 12:
                        copy_o(b, 0)
                    for name in [n for j, n in body_steps(b) if j == i]:
                        nxt = name in ("xT", "q", "k", "V", "m0")
                        if nxt:
                            evacuate(name, b + 1, 1 - p)
                        elif name[0] == "m":
                            evacuate(name, b, p)
                        else:
                            evacuate(name, b - 1, 1 - p)

            batches(act, body)
            copy_o(B - 1, 1)
            for _, name in POST:
                evacuate(name, B - 1, 1)

            def copy_wT(f, p):
                act.wait_ge(ff_filled, ff_side_of("wT", f))
                nc.scalar.copy(wT[:, p, :], SIDE[0:2 * E, :]).then_inc(ff_drained, 1)

            def hidden_hi(f, m):
                n = f * CH + m
                act.wait_ge(gelu_done, n + 1)
                if not (isinstance(n, int) and n < 4):
                    act.wait_ge(w2_done, n - 3)
                nc.scalar.copy(KS[:, 0, m % 4, :], hf[m % 4]).then_inc(hhi_done, 1)

            def ff_body(f, p):
                for m in range(CH):
                    n = f * CH + m
                    act.wait_ge(h_filled, n + 1)
                    if not (isinstance(n, int) and n < 4):
                        act.wait_ge(hlo_done, n - 3)
                    nc.scalar.activation(hf[m % 4], HB[m % 4][:], ACT.Gelu, bias=b1T[:, m:m + 1]).then_inc(gelu_done, 1)
                    if m >= 1:
                        hidden_hi(f, m - 1)
                    elif not is_at(f, 0):
                        hidden_hi(f - 1, CH - 1)
                    if m % NCH == 1:
                        e = m // NCH
                        act.wait_ge(wb_filled, f * E + e + 1)
                        if not (is_at(f, 0) and e < 2):
                            act.wait_ge(scaled, f * E + e - 1)
                        nc.scalar.copy(wb_sb[e % 2], WB[:]).then_inc(wb_copied, 1)
                    if m == 17 and not is_at(f, B - 1):
                        copy_wT(f + 1, 1 - p)

            copy_wT(0, 0)
            batches(act, ff_body)
            hidden_hi(B - 1, CH - 1)

        @block.vector
        def _(dve):
            nc.vector.memset(zero_row[:], 0.0)
            nc.vector.memset(one_row, 1.0)
            for e in range(E):
                nc.vector.memset(rank[:, e:e + 1], float(E - e))
            nc.vector.memset(KS[:, 0].bitcast(FP32), 0.0)
            nc.vector.memset(OP[0][:], 0.0)
            nc.vector.memset(OP[1][:], 0.0)
            nc.vector.memset(QS[:, 0].bitcast(FP32), 0.0)
            dve.wait_ge(cleared_pool, 1)
            for p in range(2):
                for t in range(2):
                    last = nc.vector.memset(VA[:, p, :, t::2, VW * t + DH:VW * (t + 1)], 1.0)
            last.then_inc(cleared_dve, 1)
            dve.wait_ge(const_in, 16 * 7)
            nc.vector.tensor_copy(idb[:], idf[:]).then_inc(idb_ready, 1)

            def chain(sem_, before, per):
                k = [0]

                def step(ins):
                    k[0] += 1
                    ins.then_inc(sem_, 1)
                    dve.wait_ge(sem_, before + k[0])
                    assert k[0] <= per
                return step

            def low_part(name, b):
                j = "qk".index(name)
                dve.wait_ge(hi_ready, b * 2 + j + 1)
                nc.vector.tensor_tensor(split[:, 2 * j + 1, :], SIDE[:], split[:, 2 * j, :].bitcast(FP32),
                                        ALU.subtract).then_inc(side_drained, 1)

            def maxima(b, p, s, g, first):
                if first:
                    dve.wait_ge(mask_in, 16 * 5)
                u = b * UNITS + s
                if g == 0 and not (isinstance(u, int) and u < 2):
                    s2 = (s + 2) % UNITS
                    dve.wait_ge(side_filled, side_of(f"m{s2}", b if s >= 2 else b - 1))
                for c in range(NC3):
                    n = b * (SLOTS * NC3) + (G * s + g) * NC3 + c
                    dve.wait_ge(smax_filled, n + 1)
                    own_wait(nc.vector)
                    for qb, at in QUERY_CHUNKS[c]:
                        w = (qb + 1) * P
                        sm = SM[(g + c) % 2][:, at:at + w]
                        last = nc.vector.tensor_tensor_reduce(
                            out=sm, in0=sm, in1=mask_q[:, S - w:S], scale=1.0,
                            scalar=BELOW, op0=ALU.add, op1=ALU.max, accum_out=mx[:, s % 2, qb, g:g + 1])
                    last.then_inc(smax_read, 1)

            def layer_norm(src, dst, step, count):
                for k in range(NB):
                    last = nc.vector.bn_stats(stats[:, k, :], src[:, k, :])
                step(last)
                own_wait(nc.vector)
                for k in range(NB):
                    last = nc.vector.bn_aggr(mean_var[:, k, :], stats[:, k, :])
                step(last)
                nc.vector.tensor_scalar_add(var_eps[:], mean_var[:, :, 1], EPS).then_inc(var_ready, 1)
                dve.wait_ge(rstd_ready, count + 1)
                for k in range(NB):
                    last = nc.vector.tensor_scalar(dst[:, k, :], src[:, k, :], mean_var[:, k, 0:1], rstd[:, k:k + 1],
                                                   ALU.subtract, ALU.mult)
                return last

            def post(name, b):
                dve.wait_ge(side_filled, side_of(name, b))
                if name in ("OA", "OB"):
                    half = "OA OB".split().index(name)
                    step = chain(norm_step, b * 2 + half, 1)
                    o = SIDE[:].rearrange("p (k g w) -> p k g w", k=NB, g=G)
                    step(nc.vector.reciprocal(rec[:, half], o[:, :, :, DH:2 * VW:VW]))
                    a = att[:].rearrange("p k (g s d) -> p k g s d", g=G, s=UNITS)
                    for t in range(2):
                        last = nc.vector.tensor_tensor(
                            a[:, :, :, 2 * half + t, :], o[:, :, :, VW * t:VW * t + DH],
                            rec[:, half, :, :, t].unsqueeze(3).broadcast_to([P, NB, G, DH]), ALU.mult)
                    last.then_inc(side_drained, 1)
                elif name == "proj":
                    step = chain(ln_step, b * 2, 2)
                    dve.wait_ge(xres_loaded, (b + 1) * 16)
                    last = nc.vector.tensor_tensor(y[:], SIDE[:].rearrange("p (k d) -> p k d", k=NB), y[:], ALU.add)
                    last.then_inc(side_drained, 1)
                    dve.wait_ge(side_drained, side_of(name, b))
                    layer_norm(y, y, step, b).then_inc(y_ready, 1)
                elif name == "gate":
                    step = chain(gate_step, b * GATE_STEPS, GATE_STEPS)
                    flat = lambda a: a.rearrange("p k e -> p (k e)")
                    wide = lambda a: a.unsqueeze(2).broadcast_to([P, NB, E])
                    per_e = lambda a: a[:, :].unsqueeze(1).broadcast_to([P, NB, E])
                    V = nc.vector
                    if not is_at(b, 0):
                        dve.wait_ge(kept, b * 2 + 1)
                    V.tensor_tensor(gt[:, 0], SIDE[:, 0:NB * E].rearrange("p (k e) -> p k e", k=NB), per_e(gbias),
                                    ALU.add).then_inc(side_drained, 1)
                    dve.wait_ge(side_drained, side_of(name, b))
                    step(V.tensor_reduce(gs[:, 0, :], gt[:, 0], AX.X, ALU.max))
                    step(V.tensor_tensor(gt[:, 1], gt[:, 0], wide(gs[:, 0, :]), ALU.is_equal))
                    step(V.tensor_tensor(gt[:, 2], gt[:, 1], per_e(rank), ALU.mult))
                    step(V.tensor_reduce(gs[:, 1, :], gt[:, 2], AX.X, ALU.max))
                    step(V.tensor_tensor(gt[:, 3], gt[:, 2], wide(gs[:, 1, :]), ALU.is_equal))
                    step(V.scalar_tensor_tensor(out=flat(gt[:, 1]), in0=flat(gt[:, 3]), scalar=BELOW, in1=flat(gt[:, 0]),
                                                op0=ALU.mult, op1=ALU.add))
                    step(V.tensor_reduce(gs[:, 2, :], gt[:, 1], AX.X, ALU.max))
                    step(V.tensor_tensor(gs[:, 4, :], gs[:, 2, :], gs[:, 0, :], ALU.subtract))
                    step(V.tensor_tensor(gt[:, 2], gt[:, 1], wide(gs[:, 2, :]), ALU.is_equal))
                    step(V.tensor_tensor(gt[:, 4], gt[:, 2], per_e(rank), ALU.mult))
                    step(V.tensor_reduce(gs[:, 3, :], gt[:, 4], AX.X, ALU.max))
                    step(V.tensor_tensor(gt[:, 5], gt[:, 4], wide(gs[:, 3, :]), ALU.is_equal))
                    dve.wait_ge(gexp_ready, b + 1)
                    step(V.tensor_scalar_add(gs[:, 6, :], gs[:, 5, :], 1.0))
                    step(V.reciprocal(gs[:, 7, :], gs[:, 6, :]))
                    step(V.tensor_tensor(gs[:, 6, :], gs[:, 5, :], gs[:, 7, :], ALU.mult))
                    step(V.tensor_tensor(gt[:, 1], gt[:, 3], wide(gs[:, 7, :]), ALU.mult))
                    step(V.tensor_tensor(gt[:, 2], gt[:, 5], wide(gs[:, 6, :]), ALU.mult))
                    step(V.tensor_tensor(gt[:, 0], gt[:, 1], gt[:, 2], ALU.add))
                    step(V.tensor_copy(w_hl[:, :, 0, :], gt[:, 0]))
                    V.tensor_tensor(w_hl[:, :, 1, :], gt[:, 0], w_hl[:, :, 0, :].bitcast(FP32),
                                    ALU.subtract).then_inc(w_ready, 1)

            low_part("q", 0)
            low_part("k", 0)
            for s in range(2):
                for g in range(G):
                    maxima(0, 0, s, g, s + g == 0)

            def body(b, p):
                for i in range(SLOTS):
                    s, g = divmod(i, G)
                    if not (is_at(b, B - 1) and s >= 2):
                        maxima(*unit_of(b, p, s + 2), g, False)
                    for name in [n for j, n in body_steps(b) if j == i]:
                        if name in ("q", "k"):
                            low_part(name, b + 1)
                        elif name in ("OA", "OB", "proj", "gate"):
                            post(name, b - 1)

            batches(dve, body)
            for name in ("OA", "OB", "proj", "gate"):
                post(name, B - 1)

            def take_w(f):
                dve.wait_ge(kept, (f + 1) * 2 + 1)
                nc.vector.tensor_copy(w_tok[:].rearrange("p k t e -> p (k t e)"),
                                      w_all[:, bass.ds(f, 1)].rearrange("p o k t e -> p (o k t e)")).then_inc(wtok_ready, 1)

            def yT_of(f):
                return yT_all[:, bass.ds(f, 1), :].rearrange("p o c -> p (o c)")

            def split_y(f, p):
                nc.vector.tensor_copy(split[:, 2 * p, :], yT_of(f)).then_inc(y_split, 1)
                dve.wait_ge(y_split, f * 2 + 1)
                nc.vector.tensor_tensor(split[:, 2 * p + 1, :], yT_of(f), split[:, 2 * p, :].bitcast(FP32),
                                        ALU.subtract).then_inc(y_split, 1)

            def start_sum(f, p):
                dve.wait_ge(ff_filled, ff_side_of("b2", f))
                nc.vector.tensor_tensor(acc[p], SIDE[:], yT_of(f), ALU.add).then_inc(ff_drained, 1)

            def split_w(e):
                if e == 0:
                    dve.wait_ge(w1_in, 16)
                dve.wait_ge(w2_in[e], 16)
                for j, w, done in ((0, W1[:, e, :], w1_split), (1, prf[:, S * (12 + e):S * (13 + e)], w2_split)):
                    nc.vector.tensor_copy(QS[:, j, 2 * e, :], w).then_inc(done, 1)
                    dve.wait_ge(done, 2 * e + 1)
                    nc.vector.tensor_tensor(QS[:, j, 2 * e + 1, :], w, QS[:, j, 2 * e, :].bitcast(FP32),
                                            ALU.subtract).then_inc(done, 1)

            def weigh(f, e):
                dve.wait_ge(w2_done, f * CH + (e + 1) * NCH)
                dve.wait_ge(wb_copied, f * E + e + 1)
                if not (is_at(f, 0) and e < 2):
                    dve.wait_ge(added, f * E + e - 1)
                nc.vector.tensor_tensor(part[e % 2], OE[e % 2][:], wb_sb[e % 2], ALU.mult).then_inc(scaled, 1)

            def finish(f, p):
                dve.wait_ge(ff_filled, ff_side_of("out", f))
                dve.wait_ge(out_in, (f + 1) * 16)
                step = chain(ff_step, f * 2, 2)
                dst = out_sb[p].rearrange("p (k d) -> p k d", k=NB)
                layer_norm(SIDE[:].rearrange("p (k d) -> p k d", k=NB), dst, step, f + B).then_inc(ff_drained, 1)

            def ff_body(f, p):
                for m in range(CH):
                    n = f * CH + m
                    if is_at(f, 0) and m % NCH == 0 and m // NCH + 1 < E:
                        split_w(m // NCH + 1)
                    dve.wait_ge(hhi_done, n + 1)
                    nc.vector.tensor_tensor(KS[:, 1, m % 4, :], hf[m % 4], KS[:, 0, m % 4, :].bitcast(FP32),
                                            ALU.subtract).then_inc(hlo_done, 1)
                    if m % NCH == 2:
                        e = m // NCH - 1
                        if e >= 0:
                            weigh(f, e)
                        elif not is_at(f, 0):
                            weigh(f - 1, E - 1)
                    if m == 11 and not is_at(f, 0):
                        finish(f - 1, 1 - p)
                    if not is_at(f, B - 1):
                        if m == 14:
                            dve.wait_ge(ff_filled, ff_side_of("wT", f))
                            take_w(f + 1)
                        if m == 21:
                            start_sum(f + 1, 1 - p)
                        if m == 24:
                            split_y(f + 1, 1 - p)

            take_w(0)
            split_y(0, 0)
            split_w(0)
            start_sum(0, 0)
            batches(dve, ff_body)
            weigh(B - 1, E - 1)
            finish(B - 1, 1)

        @block.tensor
        def _(pe):
            mm = nc.tensor.matmul

            def side(name, b):
                pe.wait_ge(side_drained, side_of(name, b) - 1)

            def blocks(k):
                return slice(k * P, (k + 1) * P)

            def side_step(name, b):
                side(name, b)
                if name == "xT":
                    pe.wait_ge(x_loaded, (b + 1) * 16)
                    for k in range(NB):
                        last = nc.tensor.transpose(SIDE[:, blocks(k)], x_in[:, k, :], idf[:])
                elif name in ("q", "k"):
                    last = mm(SIDE[:], WT[:, "qk".index(name), :], T[:], start=True, stop=True)
                elif name == "V":
                    for k in range(NB):
                        last = mm(SIDE[:, blocks(k)], T[:, blocks(k)], WT[:, 2, :], start=True, stop=True)
                elif name[0] == "m":
                    s = int(name[1])
                    pe.wait_ge(smax_read, (b * UNITS + s + 1) * (G * NC3))
                    for k in range(NB):
                        last = nc.tensor.transpose(SIDE[0:G, blocks(k)], mx[:, s % 2, k, :], idf[:])
                elif name in ("OA", "OB"):
                    half = "OA OB".split().index(name)
                    pe.wait_ge(o_copied, b * 2 + half + 1)
                    for k in range(NB):
                        last = nc.tensor.transpose(SIDE[:, blocks(k)], O_sb[:, half, blocks(k)], idf[:])
                elif name == "AT":
                    for k in range(NB):
                        last = nc.tensor.transpose(SIDE[:, blocks(k)], att[:, k, :], idf[:])
                elif name == "proj":
                    for k in range(NB):
                        last = mm(SIDE[:, blocks(k)], T[:, blocks(k)], WT[:, 3, :], start=True, stop=True)
                elif name == "yT":
                    pe.wait_ge(y_ready, b + 1)
                    for k in range(NB):
                        last = nc.tensor.transpose(SIDE[:, blocks(k)], y[:, k, :], idf[:])
                elif name == "gate":
                    for k in range(NB):
                        last = mm(SIDE[:, k * E:(k + 1) * E], T[:, blocks(k)], gwT[:], start=True, stop=True)
                last.then_inc(side_filled, 1)

            def scores_for_max(b, p, s, g):
                for c in range(NC3):
                    n = b * (SLOTS * NC3) + (G * s + g) * NC3 + c
                    if not (isinstance(n, int) and n < 2):
                        pe.wait_ge(smax_read, n - 1)
                    for qb, at in QUERY_CHUNKS[c]:
                        w = (qb + 1) * P
                        last = mm(SM[(g + c) % 2][:, at:at + w], QS[:, p, G * g + s, blocks(qb)], KS[:, p, s, 0:w],
                                  start=True, stop=True)
                    last.then_inc(smax_filled, 1)

            def scores(b, p, s, g):
                for c in range(NC3):
                    n = b * (SLOTS * NC3) + (G * s + g) * NC3 + c
                    if not (isinstance(n, int) and n < 3):
                        pe.wait_ge(exp_done, n - 2)
                    for kb, at in KEY_CHUNKS[c]:
                        w = S - kb * P
                        mm(ST[c][:, at:at + w], KS[:, p, s, blocks(kb)], QS[:, p, G * g + s, kb * P:S],
                           start=True, stop=False)
                        last = mm(ST[c][:, at:at + w], idb[:], mask_k[:, 0:w], start=False, stop=True)
                    last.then_inc(st_filled, 1)

            def outputs(b, p, s, kb):
                if kb == 0:
                    pe.wait_ge(exp_done, (b * UNITS + s + 1) * (G * NC3))
                    if s == 0:
                        pe.wait_ge(side_drained, side_of("V", b))
                    if s % 2 == 0 and not is_at(b, 0):
                        pe.wait_ge(o_copied, b * 2 - 1 + s // 2)
                for g in range(G):
                    last = mm(OP[s // 2][32 * g:32 * g + 2 * VW, kb * P:S], VA[:, p, kb, G * g + s, :],
                              PR[:, s % 2, g, OFF[kb]:OFF[kb] + S - kb * P],
                              start=(s % 2 == 0 and kb == 0), stop=(s % 2 == 1 and kb == NB - 1), skip_group_check=True)
                if kb == NB - 1:
                    last.then_inc(pv_done, 1)

            pe.wait_ge(const_in, 16 * 7)
            for i in range(4):
                if i:
                    pe.wait_ge(side_drained, i)
                nc.tensor.transpose(SIDE[:, 0:D], wrows[:, i, :], idf[:]).then_inc(side_filled, 1)
            pe.wait_ge(side_drained, 4)
            nc.tensor.transpose(SIDE[:, 0:E], grows[0:E, :], idf[0:E, 0:E]).then_inc(side_filled, 1)
            pe.wait_ge(side_drained, 5)
            nc.tensor.transpose(SIDE[:, 0:CH], grows[32:32 + CH, :], idf[32:32 + CH, 32:32 + CH]).then_inc(side_filled, 1)
            for name in START[6:10]:
                side_step(name, 0)
            pe.wait_ge(stack_in, STACK_IN)
            pe.wait_ge(ones_in, 16 * 2 * G)
            for s in range(2):
                for g in range(G):
                    scores_for_max(0, 0, s, g)
            side_step("m0", 0)
            pe.wait_ge(mask_in, 16 * 5)
            pe.wait_ge(idb_ready, 1)
            pe.wait_ge(cleared_dve, 1)

            def body(b, p):
                for i in range(SLOTS):
                    s, g = divmod(i, G)
                    if g == 0:
                        pe.wait_ge(mrow_in, (b * UNITS + s + 1) * (16 * G))
                    scores(b, p, s, g)
                    if not (is_at(b, B - 1) and s >= 2):
                        if i == 8:
                            pe.wait_ge(stack_in, (b + 2) * STACK_IN)
                        scores_for_max(*unit_of(b, p, s + 2), g)
                    if s:
                        outputs(b, p, s - 1, g)
                    elif not is_at(b, 0):
                        outputs(b - 1, 1 - p, UNITS - 1, g)
                    for name in [n for j, n in body_steps(b) if j == i]:
                        if name in ("xT", "q", "k", "V", "m0"):
                            side_step(name, b + 1)
                        elif name[0] == "m":
                            side_step(name, b)
                        else:
                            side_step(name, b - 1)

            batches(pe, body)
            for kb in range(NB):
                outputs(B - 1, 1, UNITS - 1, kb)
            for _, name in POST:
                side_step(name, B - 1)

            def weights_T(f, p):
                pe.wait_ge(ff_drained, ff_side_of("wT", f) - 1)
                pe.wait_ge(wtok_ready, f + 1)
                for k in range(NB):
                    last = nc.tensor.transpose(SIDE[0:2 * E, blocks(k)], w_tok[:, k].rearrange("p t e -> p (t e)"), idf[:])
                last.then_inc(ff_filled, 1)

            def biases(f, p):
                pe.wait_ge(ff_drained, ff_side_of("b2", f) - 1)
                mm(SIDE[:], b2s[:], wT[:, p, :].bitcast(FP32), start=True, stop=True).then_inc(ff_filled, 1)

            def result(f, p):
                pe.wait_ge(ff_drained, ff_side_of("out", f) - 1)
                pe.wait_ge(added, (f + 1) * E)
                for k in range(NB):
                    last = nc.tensor.transpose(SIDE[:, blocks(k)], acc[p][:, blocks(k)], idf[:])
                last.then_inc(ff_filled, 1)

            def spread(f, p, e):
                if not (is_at(f, 0) and e == 0):
                    pe.wait_ge(wb_copied, f * E + e)
                mm(WB[:], sel[:, e, :], wT[:, p, :], start=True, stop=True).then_inc(wb_filled, 1)

            def first_product(f, p, m):
                e, c = divmod(m, NCH)
                n = f * CH + m
                if m == 0:
                    pe.wait_ge(y_split, (f + 1) * 2)
                if is_at(f, 0) and c == 0:
                    pe.wait_ge(w1_split, 2 * (e + 1))
                if not (isinstance(n, int) and n < 4):
                    pe.wait_ge(gelu_done, n - 3)
                for k, (a, b_) in enumerate(((0, 0), (0, 1), (1, 0))):
                    last = mm(HB[m % 4][:], QS[:, 0, 2 * e + a, c * P:(c + 1) * P], split[:, 2 * p + b_, :],
                              start=(k == 0), stop=(k == 2))
                last.then_inc(h_filled, 1)

            def second_product(f, m):
                e, c = divmod(m, NCH)
                pe.wait_ge(hlo_done, f * CH + m + 1)
                if is_at(f, 0) and c == 0:
                    pe.wait_ge(w2_split, 2 * (e + 1))
                if c == 0 and not (is_at(f, 0) and e < 2):
                    pe.wait_ge(scaled, f * E + e - 1)
                for k, (a, b_) in enumerate(((0, 0), (0, 1), (1, 0))):
                    last = mm(OE[e % 2][:], QS[:, 1, 2 * e + a, c * P:(c + 1) * P], KS[:, b_, m % 4, :],
                              start=(c == 0 and k == 0), stop=(c == NCH - 1 and k == 2))
                last.then_inc(w2_done, 1)

            def ff_body(f, p):
                for m in range(CH):
                    if m % NCH == 0:
                        spread(f, p, m // NCH)
                    first_product(f, p, m)
                    if m >= LAG:
                        second_product(f, m - LAG)
                    elif not is_at(f, 0):
                        second_product(f - 1, CH + m - LAG)
                    if m == 10 and not is_at(f, 0):
                        result(f - 1, 1 - p)
                    if not is_at(f, B - 1):
                        if m == 16:
                            weights_T(f + 1, 1 - p)
                        if m == 20:
                            biases(f + 1, 1 - p)

            weights_T(0, 0)
            biases(0, 0)
            pe.wait_ge(sel_ready, 1)
            batches(pe, ff_body)
            for m in range(CH - LAG, CH):
                second_product(B - 1, m)
            result(B - 1, 1)


GATE_STEPS = 19
GATE_EXP = 8


def kernel(**inputs):
    import numpy as np
    import concourse.bacc as bacc
    from concourse import mybir as my
    from concourse.bass_utils import run_bass_kernel_spmd

    import ml_dtypes
    i = np.arange(P)[:, None]
    j = np.arange(P)[None, :]

    def allowed(d):
        far = i + d * P - j
        return ((far >= 0) & (far < WINDOW)) | ((far >= WINDOW + DILATION) & (far % DILATION == 0))

    masks = [np.where(allowed(d), 0.0, MASKED).astype(ml_dtypes.bfloat16) for d in (0, 1, 2, 3)]
    maskq = np.concatenate(masks[::-1], axis=1)
    maskk = np.concatenate([np.ascontiguousarray(m.T) for m in masks], axis=1)
    ident = np.eye(P, dtype=np.float32)
    select = np.repeat(np.tile(np.eye(E, dtype=np.float32), (2, 1)), P, axis=1)

    data = {k: np.ascontiguousarray(inputs[k]) for k in INPUTS}
    data.update(maskq=maskq, maskk=maskk, ident=ident, select=select)
    nc = bacc.Bacc("TRN2", target_bir_lowering=False, num_devices=1)
    aps = [nc.dram_tensor(f"in_{k}", v.shape, my.dt.from_np(v.dtype), kind="ExternalInput").ap() for k, v in data.items()]
    out = nc.dram_tensor("out", (B, S, D), FP32, kind="ExternalOutput").ap()
    build(nc, *aps, out)
    r = run_bass_kernel_spmd(nc, [{f"in_{k}": v for k, v in data.items()}], core_ids=[0])
    return r.results[0]["out"]


INPUTS = ["L0_attn_x", "L0_attn_qkv", "L0_attn_wo", "L0_ffn_gate_w", "L0_ffn_gate_b", "L0_ffn_w1", "L0_ffn_b1",
          "L0_ffn_w2", "L0_ffn_b2"]
```

```python
from contextlib import ExitStack

import concourse.bass as bass
from concourse import mybir

FP32 = mybir.dt.float32
FP32R = mybir.dt.float32r
BF16 = mybir.dt.bfloat16
ALU = mybir.AluOpType
ACT = mybir.ActivationFunctionType
AX = mybir.AxisListType

B, S, D = 8, 512, 128
H, DH = 16, 8
P = 128
NB = S // P
TB = B * NB
WINDOW, DILATION = 128, 4
E, FH = 8, 512
NCH = FH // P
CH = E * NCH
EPS = 1e-5
SCALE = float(DH) ** -0.5
MASKED = -1e30
BELOW = -3e38

G = 4
UNITS = 4
SLOTS = G * UNITS
ROW_M = 24
FAR = DILATION
ROWS = ROW_M + 1 + FAR
VW = DH + 1
OFF = [0, 512, 896, 1152]
PW = 1280
KEY_CHUNKS = [[(0, 0)], [(1, 0)], [(2, 0), (3, 256)]]
CHUNK_AT = [0, 512, 896, 1280]
QUERY_CHUNKS = [[(3, 0)], [(2, 0), (0, 384)], [(1, 0)]]
NC3 = 3

PREP = [(0, "xT"), (2, "q"), (3, "k"), (10, "V")]
POST = [(4, "OA"), (6, "OB"), (7, "AT"), (8, "proj"), (12, "yT"), (14, "gate")]
MAXES = [(1, "m1"), (5, "m2"), (9, "m3"), (13, "m0")]
BODY_FIRST = sorted(PREP + MAXES)
BODY_MID = sorted(PREP + MAXES + POST)
BODY_LAST = sorted(MAXES[:3] + POST)
START = ["w0", "w1", "w2", "w3", "gw", "b1", "xT", "q", "k", "V", "m0"]
BASE_MID = len(START) + len(BODY_FIRST)
BASE_LAST = BASE_MID + len(BODY_MID) * (B - 2)
BASE_TAIL = BASE_LAST + len(BODY_LAST)


def is_at(b, n):
    return isinstance(b, int) and b == n


def body_steps(b):
    return BODY_FIRST if is_at(b, 0) else BODY_LAST if is_at(b, B - 1) else BODY_MID


def in_body(b, name):
    k = [n for _, n in body_steps(b)].index(name) + 1
    if is_at(b, 0):
        return len(START) + k
    if is_at(b, B - 1):
        return BASE_LAST + k
    return BASE_MID + len(BODY_MID) * (b - 1) + k


def side_of(name, b):
    if name in ("xT", "q", "k", "V", "m0"):
        return START.index(name) + 1 if is_at(b, 0) else in_body(b - 1, name)
    if name in ("m1", "m2", "m3"):
        return in_body(b, name)
    if is_at(b, B - 1):
        return BASE_TAIL + [n for _, n in POST].index(name) + 1
    return in_body(b + 1, name)


FF_POST = [(10, "out")]
FF_PREP = [(20, "wT"), (24, "b2")]
FINISH_AT = [12, 13, 16, 17]
LAG = 3


def ff_side_of(name, f):
    if name == "out":
        return 3 * B if is_at(f, B - 1) else 2 + 2 + 3 * f + 1
    k = 1 if name == "wT" else 2
    if is_at(f, 0):
        return k
    if is_at(f, 1):
        return 2 + k
    return 2 + 2 + 3 * (f - 2) + 1 + k


def build(nc, x, qkv, wo, gate_w, gate_b, w1, b1, w2, b2, maskq, maskk, stack_rows, ident, select, out):
    ctx = ExitStack()
    with ctx:
        def sb(name, shape, dt=FP32):
            return ctx.enter_context(nc.sbuf_tensor(name, shape, dt))

        def pb(name):
            return ctx.enter_context(nc.psum_tensor(name, [P, S], FP32))

        def sem(name):
            return ctx.enter_context(nc.semaphore(name))

        QS = sb("QS", [P, 2, H, S], FP32R)
        KS = sb("KS", [P, 2, UNITS, S], FP32R)
        split = sb("split", [P, 4, S], FP32R)
        PR = sb("PR", [P, 2, G, PW])
        VA = sb("VA", [P, 2, NB, H, 2 * VW])
        yT_all = sb("yT_all", [P, B, S])
        logits = sb("logits", [P, TB, E])
        w_all = sb("w_all", [P, TB, 2, E], FP32R)
        W1 = sb("W1", [P, E, FH])
        x_in = sb("x_in", [P, NB, D])
        y = sb("y", [P, NB, D])
        xT = sb("xT", [P, S])
        T = sb("T", [P, S])
        O_sb = sb("O_sb", [P, 2, S])
        att = sb("att", [P, NB, D])
        mask_q = sb("mask_q", [P, S], BF16)
        mask_k = sb("mask_k", [P, S], BF16)
        idf = sb("idf", [P, P])
        idb = sb("idb", [P, P], BF16)
        sel = sb("sel", [2 * E, E, P], FP32R)
        wrows = W1[:, 4, :].rearrange("p (i d) -> p i d", i=4)
        grows = W1[:, 6, 0:P]
        select_in = W1[0:2 * E, 0:2, :].rearrange("j a c -> j (a c)")
        WT = sb("WT", [P, 4, D])
        gwT = sb("gwT", [P, E])
        b1T = sb("b1T", [P, CH])
        b2s = sb("b2s", [2 * E, D])
        gbias = sb("gbias", [P, E])
        rank = sb("rank", [P, E])
        mx = sb("mx", [P, 2, NB, G])
        rec = sb("rec", [P, 2, NB, G, 2])
        stats = sb("stats", [P, NB, 6])
        mean_var = sb("mean_var", [P, NB, 2])
        var_eps = sb("var_eps", [P, NB])
        rstd = sb("rstd", [P, NB])
        minus_half = sb("minus_half", [P, NB])
        gs = sb("gs", [P, 8, TB])
        w_tok = sb("w_tok", [P, NB, 2, E])
        wT = sb("wT", [2 * E, 2, S], FP32R)
        m_row = wT[0:G, :, :]

        ST = [pb(f"ST{i}") for i in range(3)]
        SM = [pb(f"SM{i}") for i in range(2)]
        OP = [pb(f"OP{i}") for i in range(2)]
        SIDE = pb("SIDE")
        HB = ST + [OP[1]]
        OE = SM
        WB = OP[0]

        scratch = nc.dram_tensor("scratch", [2, ROWS * H, S], FP32, kind="Internal").ap()

        const_in, mask_in, w1_in = sem("const_in"), sem("mask_in"), sem("w1_in")
        x_loaded, xres_loaded = sem("x_loaded"), sem("xres_loaded")
        w2_in = [sem(f"w2_in{e}") for e in range(E)]
        cleared_dve, cleared_pool, idb_ready = sem("cleared_dve"), sem("cleared_pool"), sem("idb_ready")
        side_filled, side_drained = sem("side_filled"), sem("side_drained")
        hi_ready, scratch_in, stack_in, mrow_in = sem("hi_ready"), sem("scratch_in"), sem("stack_in"), sem("mrow_in")
        smax_filled, smax_read = sem("smax_filled"), sem("smax_read")
        st_filled, exp_done, masked, pv_done, o_copied = sem("st_filled"), sem("exp_done"), sem("masked"), sem("pv_done"), sem("o_copied")
        norm_step, ln_step, y_ready = sem("norm_step"), sem("ln_step"), sem("y_ready")
        gate_step, gexp_ready, gdiff_ready, kept = sem("gate_step"), sem("gexp_ready"), sem("gdiff_ready"), sem("kept")
        w1_split, w2_split, y_split = sem("w1_split"), sem("w2_split"), sem("y_split")
        h_filled, gelu_done, hhi_done, hlo_done = sem("h_filled"), sem("gelu_done"), sem("hhi_done"), sem("hlo_done")
        w2_done, wb_filled, wb_copied = sem("w2_done"), sem("wb_filled"), sem("wb_copied")
        scaled, added, ff_filled, ff_drained = sem("scaled"), sem("added"), sem("ff_filled"), sem("ff_drained")
        wtok_ready, ff_step, out_in = sem("wtok_ready"), sem("ff_step"), sem("out_in")
        sel_in, sel_ready = sem("sel_in"), sem("sel_ready")
        past_wait = sem("past_wait")
        var_ready, rstd_ready = sem("var_ready"), sem("rstd_ready")

        prf = PR[:, :, :, :].rearrange("p a g c -> p (a g c)")
        hf = [prf[:, S * i:S * (i + 1)] for i in range(4)]
        wb_sb = [prf[:, S * (4 + i):S * (5 + i)] for i in range(2)]
        part = [prf[:, S * (6 + i):S * (7 + i)] for i in range(2)]
        acc = [prf[:, S * (8 + i):S * (9 + i)] for i in range(2)]
        out_sb = [prf[:, S * (10 + i):S * (11 + i)] for i in range(2)]
        W2 = [prf[:, S * (12 + e):S * (13 + e)].rearrange("p (c d) -> p c d", c=NCH) for e in range(E)]

        block = ctx.enter_context(nc.Block())

        x_v = x.rearrange("b (k p) d -> b p k d", p=P)
        out_v = out.rearrange("b (k p) d -> b p k d", p=P)
        STACK_IN = 16 * 2 * G
        SCRATCH_IN = 16 * 6

        def at_batch(v, b):
            return v[b] if isinstance(b, int) else v[bass.ds(b, 1)].rearrange("o p k d -> (o p) k d")

        def batches(eng, body):
            body(0, 0)
            with eng.Fori(0, (B - 2) // 2) as i:
                body(i * 2 + 1, 1)
                body(i * 2 + 2, 0)
            body(B - 1, 1)

        def own_wait(eng):
            eng.sem_inc(past_wait, 1)

        def unit_of(b, p, s):
            return (b, p, s) if s < UNITS else (b + 1, 1 - p, s - UNITS)

        @block.sync
        def _(sp):
            sp.dma_start(idf[:], ident[:, :]).then_inc(const_in, 16)
            for i in range(3):
                sp.dma_start(wrows[:, i, :], qkv[i * D:(i + 1) * D, :]).then_inc(const_in, 16)
            sp.dma_start(wrows[:, 3, :], wo[:, :]).then_inc(const_in, 16)
            sp.dma_start(grows[0:E, :], gate_w[:, :]).then_inc(const_in, 16)
            sp.dma_start(grows[32:64, :], b1.rearrange("e (c p) -> (e c) p", p=P)).then_inc(const_in, 16)
            sp.dma_start(x_in[:], x_v[0]).then_inc(x_loaded, 16)
            sp.dma_start(mask_q[:], maskq[:, :]).then_inc(mask_in, 16)
            sp.dma_start(mask_k[:], maskk[:, :]).then_inc(mask_in, 16)
            sp.dma_start(b2s[0:E, :], b2[:, :]).then_inc(mask_in, 16)
            sp.dma_start(b2s[E:2 * E, :], b2[:, :]).then_inc(mask_in, 16)
            sp.dma_start(gbias[:], gate_b.rearrange("(o e) -> o e", o=1).broadcast_to([P, E])).then_inc(mask_in, 16)
            sp.dma_start(select_in, select[:, :]).then_inc(sel_in, 16)
            sp.dma_start(y[:], x_v[0]).then_inc(xres_loaded, 16)

            def m_rows(b, p, s):
                sp.wait_ge(side_drained, side_of(f"m{s}", b))
                for g in range(G):
                    sp.dma_start(QS[32 * g + ROW_M:32 * g + ROW_M + 1, p, G * g + s, :].bitcast(FP32),
                                 m_row[g:g + 1, s % 2, :].bitcast(FP32)).then_inc(mrow_in, 16)

            def stacks(b, p):
                for j, name in enumerate("qk"):
                    sp.wait_ge(side_drained, side_of(name, b))
                    for t, lo in enumerate([(0, 0, 1), (0, 1, 0)][j]):
                        sp.dma_start(scratch[j, P * t:P * (t + 1)],
                                     split[:, 2 * j + lo, :].bitcast(FP32)).then_inc(scratch_in, 16)
                sp.wait_ge(scratch_in, (b + 1) * SCRATCH_IN + 32)
                for j in range(2):
                    for g in range(G):
                        rows = slice(32 * g, 32 * g + ROWS)
                        dst = KS[rows, p, :, :] if j else QS[rows, p, 4 * g:4 * g + 4, :]
                        src = scratch[j].rearrange("(r h) c -> r h c", h=H)[:, 4 * g:4 * g + 4, :]
                        sp.dma_start(dst.bitcast(FP32), src).then_inc(stack_in, 16)

            for j in range(2):
                sp.dma_start(scratch[j, 3 * P:ROWS * H], stack_rows[j]).then_inc(scratch_in, 16)
            sp.wait_ge(cleared_dve, 1)
            stacks(0, 0)
            sp.wait_ge(cleared_pool, 1)
            sp.wait_ge(side_filled, side_of("xT", 0))
            sp.dma_start(x_in[:], x_v[1]).then_inc(x_loaded, 16)
            m_rows(0, 0, 0)
            sp.wait_ge(sel_ready, 1)
            sp.dma_start(W1[:], w1.rearrange("e d f -> d e f")).then_inc(w1_in, 16)

            def body(b, p):
                m_rows(b, p, 1)
                if not is_at(b, B - 1):
                    if not is_at(b, 0):
                        sp.wait_ge(st_filled, b * (SLOTS * NC3))
                        own_wait(nc.sync)
                        sp.wait_ge(stack_in, (b + 1) * STACK_IN)
                        own_wait(nc.sync)
                    else:
                        sp.wait_ge(stack_in, STACK_IN)
                    stacks(b + 1, 1 - p)
                m_rows(b, p, 2)
                m_rows(b, p, 3)
                if not is_at(b, 0):
                    sp.wait_ge(side_filled, side_of("yT", b - 1))
                    sp.dma_start(y[:], at_batch(x_v, b)).then_inc(xres_loaded, 16)
                if not is_at(b, B - 1):
                    sp.wait_ge(side_filled, side_of("xT", b + 1))
                    own_wait(nc.sync)
                    sp.dma_start(x_in[:], at_batch(x_v, (b + 2) % B)).then_inc(x_loaded, 16)
                    m_rows(b + 1, 1 - p, 0)

            batches(sp, body)
            sp.wait_ge(pv_done, B * UNITS)
            for e in range(E):
                sp.dma_start(W2[e], w2[e].rearrange("(c p) d -> p c d", p=P)).then_inc(w2_in[e], 16)

            def store(f, p):
                sp.wait_ge(ff_drained, ff_side_of("out", f))
                sp.dma_start(at_batch(out_v, f), out_sb[p].rearrange("p (k d) -> p k d", k=NB)).then_inc(out_in, 16)

            batches(sp, store)
            sp.wait_ge(out_in, 16 * (B + 1))
            sp.wait_ge(x_loaded, 16 * (B + 1))
            sp.wait_ge(scratch_in, B * SCRATCH_IN + 32)

        @block.gpsimd
        def _(pool):
            nc.gpsimd.sem_inc(kept, 1)
            nc.gpsimd.sem_inc(out_in, 16)
            nc.gpsimd.memset(KS[:, 1].bitcast(FP32), 0.0)
            nc.gpsimd.memset(VA[:], 0.0)
            nc.gpsimd.memset(minus_half[:], -0.5)
            nc.gpsimd.memset(QS[:, 1].bitcast(FP32), 0.0).then_inc(cleared_pool, 1)

            pool.wait_ge(sel_in, 16)
            nc.gpsimd.tensor_copy(sel[:].rearrange("j e p -> j (e p)"), select_in).then_inc(sel_ready, 1)

            def mask_own(b, s):
                pool.wait_ge(exp_done, (b * UNITS + s + 1) * (G * NC3))
                own_wait(nc.gpsimd)
                for kb in range(NB):
                    own = PR[:, s % 2, :, OFF[kb]:OFF[kb] + P]
                    nc.gpsimd.affine_select(own, own, pattern=[[0, G], [1, P]], compare_op=ALU.is_ge, fill=0.0,
                                            base=0, channel_multiplier=-1).then_inc(masked, 1)

            def power(count):
                pool.wait_ge(var_ready, count + 1)
                nc.gpsimd.tensor_tensor(rstd[:], var_eps[:], minus_half[:], ALU.pow).then_inc(rstd_ready, 1)

            def normalise(f):
                power(f)
                pool.wait_ge(rstd_ready, f + 1)
                own_wait(nc.gpsimd)
                for k in range(NB):
                    last = nc.gpsimd.tensor_scalar(y[:, k, :], y[:, k, :], mean_var[:, k, 0:1], rstd[:, k:k + 1],
                                                   ALU.subtract, ALU.mult)
                last.then_inc(y_ready, 1)

            def keep(f):
                pool.wait_ge(side_drained, side_of("yT", f))
                nc.gpsimd.tensor_copy(yT_all[:, bass.ds(f, 1), :].rearrange("p o c -> p (o c)"), T[:, :]).then_inc(kept, 1)

            def body(b, p):
                mask_own(b, 0)
                mask_own(b, 1)
                if not is_at(b, 0):
                    normalise(b - 1)
                mask_own(b, 2)
                if not is_at(b, 0):
                    keep(b - 1)
                mask_own(b, 3)

            batches(pool, body)
            normalise(B - 1)
            keep(B - 1)

            def add(f, p, e):
                pool.wait_ge(scaled, f * E + e + 1)
                if e == 0:
                    pool.wait_ge(ff_drained, ff_side_of("b2", f))
                else:
                    pool.wait_ge(added, f * E + e)
                nc.gpsimd.tensor_tensor(acc[p], acc[p], part[e % 2], ALU.add).then_inc(added, 1)

            def ff_body(f, p):
                for e in range(E):
                    add(f, p, e)
                    if e == 1 and not is_at(f, 0):
                        power(f - 1 + B)

            batches(pool, ff_body)
            power(B - 1 + B)

        @block.scalar
        def _(act):
            def copy_side(dst, src, name, b, scale=None):
                act.wait_ge(side_filled, side_of(name, b))
                if scale is None:
                    return nc.scalar.copy(dst, src)
                return nc.scalar.mul(dst, src, scale)

            def evacuate(name, b, p):
                if name == "xT":
                    copy_side(xT[:], SIDE[:], name, b).then_inc(side_drained, 1)
                elif name in "qk":
                    if not is_at(b, 0):
                        act.wait_ge(scratch_in, b * SCRATCH_IN + 32)
                    copy_side(split[:, 2 * "qk".index(name), :], SIDE[:], name, b).then_inc(hi_ready, 1)
                elif name == "V":
                    if is_at(b, 0):
                        act.wait_ge(cleared_pool, 1)
                        act.wait_ge(cleared_dve, 1)
                    elif not is_at(b, 1):
                        act.wait_ge(pv_done, (b - 1) * UNITS)
                    src = SIDE[:].rearrange("p (k h t d) -> p k h t d", k=NB, t=2, d=DH)
                    for t in range(2):
                        last = copy_side(VA[:, p, :, t::2, VW * t:VW * t + DH], src[:, :, :, t, :], name, b)
                    last.then_inc(side_drained, 1)
                elif name[0] == "m":
                    s = int(name[1])
                    u = b * UNITS + s
                    if not (isinstance(u, int) and u < 2):
                        act.wait_ge(mrow_in, (u - 1) * (16 * G))
                    copy_side(m_row[:, s % 2, :], SIDE[0:G, :], name, b, -1.0).then_inc(side_drained, 1)
                elif name == "AT":
                    if not is_at(b, 0):
                        act.wait_ge(kept, b + 1)
                    copy_side(T[:], SIDE[:], name, b).then_inc(side_drained, 1)
                elif name == "yT":
                    copy_side(T[:], SIDE[:], name, b).then_inc(side_drained, 1)

            def gate_exp():
                act.wait_ge(gdiff_ready, 1)
                nc.scalar.activation(gs[:, 5, :], gs[:, 4, :], ACT.Exp).then_inc(gexp_ready, 1)

            def copy_o(b, half):
                act.wait_ge(pv_done, b * UNITS + 2 * half + 2)
                if not is_at(b, 0):
                    act.wait_ge(side_filled, side_of("OA" if half == 0 else "OB", b - 1))
                nc.scalar.copy(O_sb[:, half, :], OP[half][:]).then_inc(o_copied, 1)

            for i in range(4):
                act.wait_ge(side_filled, i + 1)
                src = SIDE[:, 0:D]
                if i < 2:
                    src = src.rearrange("p (h d) -> p d h", h=H)
                    nc.scalar.copy(WT[:, i, :].rearrange("p (d h) -> p d h", h=H), src).then_inc(side_drained, 1)
                else:
                    nc.scalar.copy(WT[:, i, :], src).then_inc(side_drained, 1)
            act.wait_ge(side_filled, 5)
            nc.scalar.copy(gwT[:], SIDE[:, 0:E]).then_inc(side_drained, 1)
            act.wait_ge(side_filled, 6)
            nc.scalar.copy(b1T[:], SIDE[:, 0:CH]).then_inc(side_drained, 1)
            for name in START[6:]:
                evacuate(name, 0, 0)

            def body(b, p):
                for i in range(SLOTS):
                    s, g = divmod(i, G)
                    u = b * UNITS + s
                    if g == 0 and not (isinstance(u, int) and u < 2):
                        act.wait_ge(pv_done, u - 1)
                    for c in range(NC3):
                        act.wait_ge(st_filled, b * (SLOTS * NC3) + i * NC3 + c + 1)
                        n = CHUNK_AT[c + 1] - CHUNK_AT[c]
                        nc.scalar.activation(PR[:, s % 2, g, CHUNK_AT[c]:CHUNK_AT[c + 1]], ST[c][:, 0:n],
                                             ACT.Exp, scale=SCALE).then_inc(exp_done, 1)
                        if c == 1:
                            for name in [n for j, n in body_steps(b) if j == i]:
                                if name in ("xT", "q", "k", "V", "m0"):
                                    evacuate(name, b + 1, 1 - p)
                                elif name[0] == "m":
                                    evacuate(name, b, p)
                                else:
                                    evacuate(name, b - 1, 1 - p)
                    if i == 4 and not is_at(b, 0):
                        copy_o(b - 1, 1)
                    if i == 12:
                        copy_o(b, 0)

            batches(act, body)
            copy_o(B - 1, 1)
            for _, name in POST:
                evacuate(name, B - 1, 1)
            gate_exp()

            def copy_wT(f, p):
                act.wait_ge(ff_filled, ff_side_of("wT", f))
                nc.scalar.copy(wT[:, p, :], SIDE[0:2 * E, :]).then_inc(ff_drained, 1)

            def hidden_hi(f, m):
                n = f * CH + m
                act.wait_ge(gelu_done, n + 1)
                if not (isinstance(n, int) and n < 4):
                    act.wait_ge(w2_done, n - 3)
                nc.scalar.copy(KS[:, 0, m % 4, :], hf[m % 4]).then_inc(hhi_done, 1)

            def ff_body(f, p):
                for m in range(CH):
                    n = f * CH + m
                    act.wait_ge(h_filled, n + 1)
                    if not (isinstance(n, int) and n < 4):
                        act.wait_ge(hlo_done, n - 3)
                    nc.scalar.activation(hf[m % 4], HB[m % 4][:], ACT.Gelu, bias=b1T[:, m:m + 1]).then_inc(gelu_done, 1)
                    if m >= 1:
                        hidden_hi(f, m - 1)
                    elif not is_at(f, 0):
                        hidden_hi(f - 1, CH - 1)
                    if m % NCH == 1:
                        e = m // NCH
                        act.wait_ge(wb_filled, f * E + e + 1)
                        if not (is_at(f, 0) and e < 2):
                            act.wait_ge(scaled, f * E + e - 1)
                        nc.scalar.copy(wb_sb[e % 2], WB[:]).then_inc(wb_copied, 1)
                    if m == 21 and not is_at(f, B - 1):
                        copy_wT(f + 1, 1 - p)

            copy_wT(0, 0)
            batches(act, ff_body)
            hidden_hi(B - 1, CH - 1)

        @block.vector
        def _(dve):
            for e in range(E):
                nc.vector.memset(rank[:, e:e + 1], float(E - e))
            nc.vector.memset(KS[:, 0].bitcast(FP32), 0.0)
            nc.vector.memset(OP[0][:], 0.0)
            nc.vector.memset(OP[1][:], 0.0)
            nc.vector.memset(QS[:, 0].bitcast(FP32), 0.0)
            dve.wait_ge(cleared_pool, 1)
            for p in range(2):
                for t in range(2):
                    last = nc.vector.memset(VA[:, p, :, t::2, VW * t + DH:VW * (t + 1)], 1.0)
            last.then_inc(cleared_dve, 1)
            dve.wait_ge(const_in, 16 * 7)
            nc.vector.tensor_copy(idb[:], idf[:]).then_inc(idb_ready, 1)

            def chain(sem_, before, per):
                k = [0]

                def step(ins):
                    k[0] += 1
                    ins.then_inc(sem_, 1)
                    dve.wait_ge(sem_, before + k[0])
                    assert k[0] <= per
                return step

            def low_part(name, b):
                j = "qk".index(name)
                dve.wait_ge(hi_ready, b * 2 + j + 1)
                nc.vector.tensor_tensor(split[:, 2 * j + 1, :], SIDE[:], split[:, 2 * j, :].bitcast(FP32),
                                        ALU.subtract).then_inc(side_drained, 1)

            def maxima(b, p, s, g, c):
                u = b * UNITS + s
                if g + c == 0 and not (isinstance(u, int) and u < 2):
                    s2 = (s + 2) % UNITS
                    dve.wait_ge(side_filled, side_of(f"m{s2}", b if s >= 2 else b - 1))
                n = b * (SLOTS * NC3) + (G * s + g) * NC3 + c
                dve.wait_ge(smax_filled, n + 1)
                own_wait(nc.vector)
                for qb, at in QUERY_CHUNKS[c]:
                    w = (qb + 1) * P
                    sm = SM[(g + c) % 2][:, at:at + w]
                    last = nc.vector.tensor_tensor_reduce(
                        out=sm, in0=sm, in1=mask_q[:, S - w:S], scale=1.0,
                        scalar=BELOW, op0=ALU.add, op1=ALU.max, accum_out=mx[:, s % 2, qb, g:g + 1])
                last.then_inc(smax_read, 1)

            def bn_stats(src, step):
                for k in range(NB):
                    last = nc.vector.bn_stats(stats[:, k, :], src[:, k, :])
                step(last)

            def variance(step):
                own_wait(nc.vector)
                for k in range(NB):
                    last = nc.vector.bn_aggr(mean_var[:, k, :], stats[:, k, :])
                step(last)
                nc.vector.tensor_scalar_add(var_eps[:], mean_var[:, :, 1], EPS).then_inc(var_ready, 1)

            def post(name, b):
                dve.wait_ge(side_filled, side_of(name, b))
                if name in ("OA", "OB"):
                    half = "OA OB".split().index(name)
                    step = chain(norm_step, b * 2 + half, 1)
                    o = SIDE[:].rearrange("p (k g w) -> p k g w", k=NB, g=G)
                    step(nc.vector.reciprocal(rec[:, half], o[:, :, :, DH:2 * VW:VW]))
                    a = att[:].rearrange("p k (g s d) -> p k g s d", g=G, s=UNITS)
                    for t in range(2):
                        last = nc.vector.tensor_tensor(
                            a[:, :, :, 2 * half + t, :], o[:, :, :, VW * t:VW * t + DH],
                            rec[:, half, :, :, t].unsqueeze(3).broadcast_to([P, NB, G, DH]), ALU.mult)
                    last.then_inc(side_drained, 1)
                elif name == "proj":
                    step = chain(ln_step, b * 2, 2)
                    dve.wait_ge(xres_loaded, (b + 1) * 16)
                    last = nc.vector.tensor_tensor(y[:], SIDE[:].rearrange("p (k d) -> p k d", k=NB), y[:], ALU.add)
                    last.then_inc(side_drained, 1)
                    dve.wait_ge(side_drained, side_of(name, b))
                    bn_stats(y, step)
                    variance(step)
                elif name == "gate":
                    nc.vector.tensor_tensor(
                        logits[:, bass.ds(b * NB, NB), :], SIDE[:, 0:NB * E].rearrange("p (k e) -> p k e", k=NB),
                        gbias[:, :].unsqueeze(1).broadcast_to([P, NB, E]), ALU.add).then_inc(side_drained, 1)

            def gate():
                step = chain(gate_step, 0, 20)
                V = nc.vector
                gt = [prf[:, S * 4 + TB * E * i:S * 4 + TB * E * (i + 1)].rearrange("p (k e) -> p k e", e=E) for i in range(5)]
                wide = lambda a: a.unsqueeze(2).broadcast_to([P, TB, E])
                ranks = rank[:, :].unsqueeze(1).broadcast_to([P, TB, E])
                dve.wait_ge(side_drained, side_of("gate", B - 1))
                dve.wait_ge(pv_done, B * UNITS)
                step(V.tensor_reduce(gs[:, 0, :], logits[:], AX.X, ALU.max))
                step(V.tensor_tensor(gt[0], logits[:], wide(gs[:, 0, :]), ALU.is_equal))
                step(V.tensor_tensor(gt[1], gt[0], ranks, ALU.mult))
                step(V.tensor_reduce(gs[:, 1, :], gt[1], AX.X, ALU.max))
                step(V.tensor_tensor(gt[2], gt[1], wide(gs[:, 1, :]), ALU.is_equal))
                step(V.tensor_scalar_mul(gt[1], gt[2], BELOW))
                step(V.tensor_tensor(gt[0], gt[1], logits[:], ALU.add))
                step(V.tensor_reduce(gs[:, 2, :], gt[0], AX.X, ALU.max))
                V.tensor_tensor(gs[:, 4, :], gs[:, 2, :], gs[:, 0, :], ALU.subtract).then_inc(gdiff_ready, 1)
                step(V.tensor_tensor(gt[1], gt[0], wide(gs[:, 2, :]), ALU.is_equal))
                step(V.tensor_tensor(gt[3], gt[1], ranks, ALU.mult))
                step(V.tensor_reduce(gs[:, 3, :], gt[3], AX.X, ALU.max))
                step(V.tensor_tensor(gt[4], gt[3], wide(gs[:, 3, :]), ALU.is_equal))
                dve.wait_ge(gexp_ready, 1)
                step(V.tensor_scalar_add(gs[:, 6, :], gs[:, 5, :], 1.0))
                step(V.reciprocal(gs[:, 7, :], gs[:, 6, :]))
                step(V.tensor_tensor(gs[:, 6, :], gs[:, 5, :], gs[:, 7, :], ALU.mult))
                step(V.tensor_tensor(gt[0], gt[2], wide(gs[:, 7, :]), ALU.mult))
                step(V.tensor_tensor(gt[1], gt[4], wide(gs[:, 6, :]), ALU.mult))
                step(V.tensor_tensor(gt[3], gt[0], gt[1], ALU.add))
                step(V.tensor_copy(w_all[:, :, 0, :], gt[3]))
                step(V.tensor_tensor(w_all[:, :, 1, :], gt[3], w_all[:, :, 0, :].bitcast(FP32), ALU.subtract))

            low_part("q", 0)
            low_part("k", 0)
            dve.wait_ge(mask_in, 16 * 5)
            for s in range(2):
                for g in range(G):
                    for c in range(NC3):
                        maxima(0, 0, s, g, c)

            def body(b, p):
                for i in range(SLOTS):
                    s, g = divmod(i, G)
                    for c in range(NC3):
                        if not (is_at(b, B - 1) and s >= 2):
                            maxima(*unit_of(b, p, s + 2), g, c)
                        if c == 1:
                            for name in [n for j, n in body_steps(b) if j == i]:
                                if name in ("q", "k"):
                                    low_part(name, b + 1)
                                elif name in ("OA", "OB", "proj", "gate"):
                                    post(name, b - 1)

            batches(dve, body)
            for name in ("OA", "OB", "proj", "gate"):
                post(name, B - 1)

            def take_w(f):
                dve.wait_ge(kept, f + 2)
                nc.vector.tensor_copy(w_tok[:].rearrange("p k t e -> p (k t e)"),
                                      w_all[:, bass.ds(f * NB, NB)].bitcast(FP32).rearrange("p k t e -> p (k t e)")).then_inc(wtok_ready, 1)

            def yT_of(f):
                return yT_all[:, bass.ds(f, 1), :].rearrange("p o c -> p (o c)")

            def split_y(f, p):
                nc.vector.tensor_copy(split[:, 2 * p, :], yT_of(f)).then_inc(y_split, 1)
                dve.wait_ge(y_split, f * 2 + 1)
                nc.vector.tensor_tensor(split[:, 2 * p + 1, :], yT_of(f), split[:, 2 * p, :].bitcast(FP32),
                                        ALU.subtract).then_inc(y_split, 1)

            def start_sum(f, p):
                dve.wait_ge(ff_filled, ff_side_of("b2", f))
                nc.vector.tensor_tensor(acc[p], SIDE[:], yT_of(f), ALU.add).then_inc(ff_drained, 1)

            def split_w(e):
                if e == 0:
                    dve.wait_ge(w1_in, 16)
                dve.wait_ge(w2_in[e], 16)
                for j, w, done in ((0, W1[:, e, :], w1_split), (1, prf[:, S * (12 + e):S * (13 + e)], w2_split)):
                    nc.vector.tensor_copy(QS[:, j, 2 * e, :], w).then_inc(done, 1)
                    dve.wait_ge(done, 2 * e + 1)
                    nc.vector.tensor_tensor(QS[:, j, 2 * e + 1, :], w, QS[:, j, 2 * e, :].bitcast(FP32),
                                            ALU.subtract).then_inc(done, 1)

            def weigh(f, e):
                dve.wait_ge(w2_done, f * CH + (e + 1) * NCH)
                dve.wait_ge(wb_copied, f * E + e + 1)
                if not (is_at(f, 0) and e < 2):
                    dve.wait_ge(added, f * E + e - 1)
                nc.vector.tensor_tensor(part[e % 2], OE[e % 2][:], wb_sb[e % 2], ALU.mult).then_inc(scaled, 1)

            def finish(f, p, steps):
                result = SIDE[:].rearrange("p (k d) -> p k d", k=NB)
                dst = out_sb[p].rearrange("p (k d) -> p k d", k=NB)
                step = chain(ff_step, f * 2 + min(steps), 2)
                if 0 in steps:
                    dve.wait_ge(ff_filled, ff_side_of("out", f))
                    bn_stats(result, step)
                if 1 in steps:
                    variance(step)
                if 2 in steps:
                    dve.wait_ge(rstd_ready, f + B + 1)
                    dve.wait_ge(out_in, (f + 1) * 16)
                for k in range(NB):
                    if 2 + k // 2 in steps:
                        last = nc.vector.tensor_scalar(dst[:, k, :], result[:, k, :], mean_var[:, k, 0:1],
                                                       rstd[:, k:k + 1], ALU.subtract, ALU.mult)
                if 3 in steps:
                    last.then_inc(ff_drained, 1)

            def ff_body(f, p):
                for m in range(CH):
                    n = f * CH + m
                    if is_at(f, 0) and m % NCH == 0 and m // NCH + 1 < E:
                        split_w(m // NCH + 1)
                    dve.wait_ge(hhi_done, n + 1)
                    nc.vector.tensor_tensor(KS[:, 1, m % 4, :], hf[m % 4], KS[:, 0, m % 4, :].bitcast(FP32),
                                            ALU.subtract).then_inc(hlo_done, 1)
                    if m % NCH == 3:
                        e = m // NCH - 1
                        if e >= 0:
                            weigh(f, e)
                        elif not is_at(f, 0):
                            weigh(f - 1, E - 1)
                    if m in FINISH_AT and not is_at(f, 0):
                        finish(f - 1, 1 - p, [FINISH_AT.index(m)])
                    if not is_at(f, B - 1):
                        if m == 18:
                            dve.wait_ge(ff_filled, ff_side_of("wT", f))
                            take_w(f + 1)
                        if m == 26:
                            start_sum(f + 1, 1 - p)
                        if m == 28:
                            split_y(f + 1, 1 - p)

            gate()
            take_w(0)
            split_y(0, 0)
            split_w(0)
            start_sum(0, 0)
            batches(dve, ff_body)
            weigh(B - 1, E - 1)
            finish(B - 1, 1, [0, 1, 2, 3])

        @block.tensor
        def _(pe):
            mm = nc.tensor.matmul

            def side(name, b):
                pe.wait_ge(side_drained, side_of(name, b) - 1)

            def blocks(k):
                return slice(k * P, (k + 1) * P)

            def side_step(name, b):
                side(name, b)
                if name == "xT":
                    pe.wait_ge(x_loaded, (b + 1) * 16)
                    for k in range(NB):
                        last = nc.tensor.transpose(SIDE[:, blocks(k)], x_in[:, k, :], idf[:])
                elif name in ("q", "k"):
                    last = mm(SIDE[:], WT[:, "qk".index(name), :], xT[:], start=True, stop=True)
                elif name == "V":
                    for k in range(NB):
                        last = mm(SIDE[:, blocks(k)], xT[:, blocks(k)], WT[:, 2, :], start=True, stop=True)
                elif name[0] == "m":
                    s = int(name[1])
                    pe.wait_ge(smax_read, (b * UNITS + s + 1) * (G * NC3))
                    for k in range(NB):
                        last = nc.tensor.transpose(SIDE[0:G, blocks(k)], mx[:, s % 2, k, :], idf[:])
                elif name in ("OA", "OB"):
                    half = "OA OB".split().index(name)
                    pe.wait_ge(o_copied, b * 2 + half + 1)
                    for k in range(NB):
                        last = nc.tensor.transpose(SIDE[:, blocks(k)], O_sb[:, half, blocks(k)], idf[:])
                elif name == "AT":
                    for k in range(NB):
                        last = nc.tensor.transpose(SIDE[:, blocks(k)], att[:, k, :], idf[:])
                elif name == "proj":
                    for k in range(NB):
                        last = mm(SIDE[:, blocks(k)], T[:, blocks(k)], WT[:, 3, :], start=True, stop=True)
                elif name == "yT":
                    pe.wait_ge(y_ready, b + 1)
                    for k in range(NB):
                        last = nc.tensor.transpose(SIDE[:, blocks(k)], y[:, k, :], idf[:])
                elif name == "gate":
                    for k in range(NB):
                        last = mm(SIDE[:, k * E:(k + 1) * E], T[:, blocks(k)], gwT[:], start=True, stop=True)
                last.then_inc(side_filled, 1)

            def scores_for_max(b, p, s, g, c):
                n = b * (SLOTS * NC3) + (G * s + g) * NC3 + c
                if not (isinstance(n, int) and n < 2):
                    pe.wait_ge(smax_read, n - 1)
                for qb, at in QUERY_CHUNKS[c]:
                    w = (qb + 1) * P
                    last = mm(SM[(g + c) % 2][:, at:at + w], QS[:, p, G * g + s, blocks(qb)], KS[:, p, s, 0:w],
                              start=True, stop=True)
                last.then_inc(smax_filled, 1)

            def scores(b, p, s, g, c):
                n = b * (SLOTS * NC3) + (G * s + g) * NC3 + c
                if not (isinstance(n, int) and n < 3):
                    pe.wait_ge(exp_done, n - 2)
                for kb, at in KEY_CHUNKS[c]:
                    w = S - kb * P
                    to = 2 * P if kb == 0 else w
                    last = mm(ST[c][:, at:at + w], KS[:, p, s, blocks(kb)], QS[:, p, G * g + s, kb * P:S],
                              start=True, stop=w == P, skip_group_check=True)
                    if to > P:
                        last = mm(ST[c][:, at + P:at + to], idb[:], mask_k[:, P:to], start=False, stop=True,
                                  skip_group_check=True)
                last.then_inc(st_filled, 1)

            def outputs(b, p, s, kb):
                pe.wait_ge(masked, (b * UNITS + s) * NB + kb + 1)
                if kb == 0:
                    if s == 0:
                        pe.wait_ge(side_drained, side_of("V", b))
                    if s % 2 == 0 and not is_at(b, 0):
                        pe.wait_ge(o_copied, b * 2 - 1 + s // 2)
                for g in range(G):
                    last = mm(OP[s // 2][32 * g:32 * g + 2 * VW, kb * P:S], VA[:, p, kb, G * g + s, :],
                              PR[:, s % 2, g, OFF[kb]:OFF[kb] + S - kb * P],
                              start=(s % 2 == 0 and kb == 0), stop=(s % 2 == 1 and kb == NB - 1), skip_group_check=True)
                if kb == NB - 1:
                    last.then_inc(pv_done, 1)

            def side_steps_of(b, i):
                for name in [n for j, n in body_steps(b) if j == i]:
                    if name in ("xT", "q", "k", "V", "m0"):
                        side_step(name, b + 1)
                    elif name[0] == "m":
                        side_step(name, b)
                    else:
                        side_step(name, b - 1)

            pe.wait_ge(const_in, 16 * 7)
            for i in range(4):
                if i:
                    pe.wait_ge(side_drained, i)
                nc.tensor.transpose(SIDE[:, 0:D], wrows[:, i, :], idf[:]).then_inc(side_filled, 1)
            pe.wait_ge(side_drained, 4)
            nc.tensor.transpose(SIDE[:, 0:E], grows[0:E, :], idf[0:E, 0:E]).then_inc(side_filled, 1)
            pe.wait_ge(side_drained, 5)
            nc.tensor.transpose(SIDE[:, 0:CH], grows[32:32 + CH, :], idf[32:32 + CH, 32:32 + CH]).then_inc(side_filled, 1)
            for name in START[6:10]:
                side_step(name, 0)
            pe.wait_ge(stack_in, STACK_IN)
            for s in range(2):
                for g in range(G):
                    for c in range(NC3):
                        scores_for_max(0, 0, s, g, c)
            side_step("m0", 0)
            pe.wait_ge(mask_in, 16 * 5)
            pe.wait_ge(idb_ready, 1)
            pe.wait_ge(cleared_dve, 1)

            def body(b, p):
                for i in range(SLOTS):
                    s, g = divmod(i, G)
                    if g == 0:
                        pe.wait_ge(mrow_in, (b * UNITS + s + 1) * (16 * G))
                    if i == 8 and not is_at(b, B - 1):
                        pe.wait_ge(stack_in, (b + 2) * STACK_IN)
                    for c in range(NC3):
                        scores(b, p, s, g, c)
                        if not (is_at(b, B - 1) and s >= 2):
                            scores_for_max(*unit_of(b, p, s + 2), g, c)
                        if c == 1:
                            side_steps_of(b, i)
                    if s:
                        outputs(b, p, s - 1, g)
                    elif not is_at(b, 0):
                        outputs(b - 1, 1 - p, UNITS - 1, g)

            batches(pe, body)
            for kb in range(NB):
                outputs(B - 1, 1, UNITS - 1, kb)
            for _, name in POST:
                side_step(name, B - 1)

            def weights_T(f, p):
                pe.wait_ge(ff_drained, ff_side_of("wT", f) - 1)
                pe.wait_ge(wtok_ready, f + 1)
                for k in range(NB):
                    last = nc.tensor.transpose(SIDE[0:2 * E, blocks(k)], w_tok[:, k].rearrange("p t e -> p (t e)"), idf[:])
                last.then_inc(ff_filled, 1)

            def biases(f, p):
                pe.wait_ge(ff_drained, ff_side_of("b2", f) - 1)
                mm(SIDE[:], b2s[:], wT[:, p, :].bitcast(FP32), start=True, stop=True).then_inc(ff_filled, 1)

            def result(f, p):
                pe.wait_ge(ff_drained, ff_side_of("out", f) - 1)
                pe.wait_ge(added, (f + 1) * E)
                for k in range(NB):
                    last = nc.tensor.transpose(SIDE[:, blocks(k)], acc[p][:, blocks(k)], idf[:])
                last.then_inc(ff_filled, 1)

            def spread(f, p, e):
                if not (is_at(f, 0) and e == 0):
                    pe.wait_ge(wb_copied, f * E + e)
                mm(WB[:], sel[:, e, :], wT[:, p, :], start=True, stop=True).then_inc(wb_filled, 1)

            def first_product(f, p, m):
                e, c = divmod(m, NCH)
                n = f * CH + m
                if m == 0:
                    pe.wait_ge(y_split, (f + 1) * 2)
                if is_at(f, 0) and c == 0:
                    pe.wait_ge(w1_split, 2 * (e + 1))
                if not (isinstance(n, int) and n < 4):
                    pe.wait_ge(gelu_done, n - 3)
                for k, (a, b_) in enumerate(((0, 0), (0, 1), (1, 0))):
                    last = mm(HB[m % 4][:], QS[:, 0, 2 * e + a, c * P:(c + 1) * P], split[:, 2 * p + b_, :],
                              start=(k == 0), stop=(k == 2))
                last.then_inc(h_filled, 1)

            def second_product(f, m):
                e, c = divmod(m, NCH)
                pe.wait_ge(hlo_done, f * CH + m + 1)
                if is_at(f, 0) and c == 0:
                    pe.wait_ge(w2_split, 2 * (e + 1))
                if c == 0 and not (is_at(f, 0) and e < 2):
                    pe.wait_ge(scaled, f * E + e - 1)
                for k, (a, b_) in enumerate(((0, 0), (0, 1), (1, 0))):
                    last = mm(OE[e % 2][:], QS[:, 1, 2 * e + a, c * P:(c + 1) * P], KS[:, b_, m % 4, :],
                              start=(c == 0 and k == 0), stop=(c == NCH - 1 and k == 2))
                last.then_inc(w2_done, 1)

            def ff_body(f, p):
                for m in range(CH):
                    if m % NCH == 0:
                        spread(f, p, m // NCH)
                    first_product(f, p, m)
                    if m >= LAG:
                        second_product(f, m - LAG)
                    elif not is_at(f, 0):
                        second_product(f - 1, CH + m - LAG)
                    if m == 10 and not is_at(f, 0):
                        result(f - 1, 1 - p)
                    if not is_at(f, B - 1):
                        if m == 20:
                            weights_T(f + 1, 1 - p)
                        if m == 24:
                            biases(f + 1, 1 - p)

            weights_T(0, 0)
            biases(0, 0)
            pe.wait_ge(sel_ready, 1)
            batches(pe, ff_body)
            for m in range(CH - LAG, CH):
                second_product(B - 1, m)
            result(B - 1, 1)




def kernel(**inputs):
    import numpy as np
    import concourse.bacc as bacc
    from concourse import mybir as my
    from concourse.bass_utils import run_bass_kernel_spmd

    import ml_dtypes
    i = np.arange(P)[:, None]
    j = np.arange(P)[None, :]

    def allowed(d):
        far = i + d * P - j
        return ((far >= 0) & (far < WINDOW)) | ((far >= WINDOW + DILATION) & (far % DILATION == 0))

    masks = [np.where(allowed(d), 0.0, MASKED).astype(ml_dtypes.bfloat16) for d in (0, 1, 2, 3)]
    maskq = np.concatenate(masks[::-1], axis=1)
    maskk = np.concatenate([np.ascontiguousarray(m.T) for m in masks], axis=1)
    token, residue = np.arange(S)[None, :], np.arange(FAR)[:, None]
    rows_q = np.where((token >= 2 * P) & (token % FAR != residue), MASKED, 0.0)
    rows_k = np.where((token < P) & (token % FAR == residue), 1.0, 0.0)
    stack_rows = np.stack([np.repeat(np.concatenate([np.full((1, S), one), rows]), H, axis=0)
                           for one, rows in ((0.0, rows_q), (1.0, rows_k))]).astype(np.float32)
    ident = np.eye(P, dtype=np.float32)
    select = np.repeat(np.tile(np.eye(E, dtype=np.float32), (2, 1)), P, axis=1)

    data = {k: np.ascontiguousarray(inputs[k]) for k in INPUTS}
    data.update(maskq=maskq, maskk=maskk, stack_rows=stack_rows, ident=ident, select=select)
    nc = bacc.Bacc("TRN2", target_bir_lowering=False, num_devices=1)
    aps = [nc.dram_tensor(f"in_{k}", v.shape, my.dt.from_np(v.dtype), kind="ExternalInput").ap() for k, v in data.items()]
    out = nc.dram_tensor("out", (B, S, D), FP32, kind="ExternalOutput").ap()
    build(nc, *aps, out)
    r = run_bass_kernel_spmd(nc, [{f"in_{k}": v for k, v in data.items()}], core_ids=[0])
    return r.results[0]["out"]


INPUTS = ["L0_attn_x", "L0_attn_qkv", "L0_attn_wo", "L0_ffn_gate_w", "L0_ffn_gate_b", "L0_ffn_w1", "L0_ffn_b1",
          "L0_ffn_w2", "L0_ffn_b2"]
```

```python
from contextlib import ExitStack

import concourse.bass as bass
from concourse import mybir

FP32 = mybir.dt.float32
FP32R = mybir.dt.float32r
BF16 = mybir.dt.bfloat16
ALU = mybir.AluOpType
ACT = mybir.ActivationFunctionType
AX = mybir.AxisListType

B, S, D = 8, 512, 128
H, DH = 16, 8
P = 128
NB = S // P
TB = B * NB
WINDOW, DILATION = 128, 4
E, FH = 8, 512
NCH = FH // P
CH = E * NCH
EPS = 1e-5
SCALE = float(DH) ** -0.5
MASKED = -1e30
BELOW = -3e38

G = 4
UNITS = 4
SLOTS = G * UNITS
ROW_M = 24
FAR = DILATION
ROWS = ROW_M + 1 + FAR
VW = DH + 1
OFF = [0, 512, 896, 1152]
PW = 1280
KEY_CHUNKS = [[(0, 0)], [(1, 0)], [(2, 0), (3, 256)]]
CHUNK_AT = [0, 512, 896, 1280]
QUERY_CHUNKS = [[(3, 0)], [(2, 0), (0, 384)], [(1, 0)]]
NC3 = 3



def place(slot, chunk=1):
    return slot * NC3 + chunk


PREP = [(place(0, 0), "xT"), (place(1), "q"), (place(2), "k"), (place(10), "V")]
POST = [(place(4), "OA"), (place(6), "OB"), (place(7), "AT"), (place(8), "proj"), (place(14), "yT"), (place(15), "gate")]
MAXES = [(place(0, 2), "m1"), (place(5), "m2"), (place(9), "m3"), (place(13), "m0")]
MOMENTS_AT = [place(9, 0), place(9, 2)]
BODY_FIRST = sorted(PREP + MAXES)
BODY_MID = sorted(PREP + MAXES + POST)
BODY_LAST = sorted(MAXES[:3] + POST)
START = ["w", "xT", "q", "k", "V", "gb", "m0"]
BASE_MID = len(START) + len(BODY_FIRST)
BASE_LAST = BASE_MID + len(BODY_MID) * (B - 2)
BASE_TAIL = BASE_LAST + len(BODY_LAST)


def is_at(b, n):
    return isinstance(b, int) and b == n


def body_steps(b):
    return BODY_FIRST if is_at(b, 0) else BODY_LAST if is_at(b, B - 1) else BODY_MID


def in_body(b, name):
    k = [n for _, n in body_steps(b)].index(name) + 1
    if is_at(b, 0):
        return len(START) + k
    if is_at(b, B - 1):
        return BASE_LAST + k
    return BASE_MID + len(BODY_MID) * (b - 1) + k


def side_of(name, b):
    if name in ("w", "gb"):
        return START.index(name) + 1
    if name in ("xT", "q", "k", "V", "m0"):
        return START.index(name) + 1 if is_at(b, 0) else in_body(b - 1, name)
    if name in ("m1", "m2", "m3"):
        return in_body(b, name)
    if is_at(b, B - 1):
        return BASE_TAIL + [n for _, n in POST].index(name) + 1
    return in_body(b + 1, name)


FF_POST = [(10, "out")]
FF_PREP = [(20, "wT"), (24, "b2")]
FINISH_AT = [12, 13, 16, 17]
FF_TAIL = [(2, "OA"), (4, "OB"), (6, "AT"), (8, "proj"), (15, "yT"), (17, "gate")]
FF_MOMENTS_AT = [9, 10]
GATE_AT = [21, 23, 25, 30]
GATE_EXP_AT = 26
W1_AT = 8
GATE_SLOTS = [12, 12, 12, 14]
GATE_EXP_SLOT = 13
GATES = [(0, (B - 2) * NB), ((B - 2) * NB, B * NB)]
GATE_STEPS = [5, 3, 4, 8]
LAG = 3


def ff_side_of(name, f):
    if name == "out":
        return 3 * B if is_at(f, B - 1) else 2 + 2 + 3 * f + 1
    k = 1 if name == "wT" else 2
    if is_at(f, 0):
        return k
    if is_at(f, 1):
        return 2 + k
    return 2 + 2 + 3 * (f - 2) + 1 + k


def build(nc, x, qkv, wo, gate_w, gate_b, w1, b1, w2, b2, maskq, maskk, stack_rows, ident, select, out):
    ctx = ExitStack()
    with ctx:
        def sb(name, shape, dt=FP32):
            return ctx.enter_context(nc.sbuf_tensor(name, shape, dt))

        def pb(name):
            return ctx.enter_context(nc.psum_tensor(name, [P, S], FP32))

        def sem(name):
            return ctx.enter_context(nc.semaphore(name))

        QS = sb("QS", [P, 2, H, S], FP32R)
        KS = sb("KS", [P, 2, UNITS, S], FP32R)
        split = sb("split", [P, 4, S], FP32R)
        PR = sb("PR", [P, 2, G, PW])
        VA = sb("VA", [P, 2, NB, H, 2 * VW])
        yT_all = sb("yT_all", [P, B, S])
        logits = sb("logits", [P, TB, E])
        w_all = sb("w_all", [P, TB, 2, E], FP32R)
        W1 = sb("W1", [P, E, FH])
        x_in = sb("x_in", [P, NB, D])
        y = sb("y", [P, NB, D])
        xT = sb("xT", [P, S])
        T = sb("T", [P, S])
        O_sb = sb("O_sb", [P, 2, S])
        att = sb("att", [P, NB, D])
        mask_q = sb("mask_q", [P, S], BF16)
        mask_k = sb("mask_k", [P, S], BF16)
        idf = sb("idf", [P, P])
        idb = sb("idb", [P, P], BF16)
        sel = sb("sel", [2 * E, E, P], FP32R)
        wrows = W1[:, 4, :].rearrange("p (i d) -> p i d", i=4)
        gate_rows, b1_rows = W1[0:E, 6, 0:P], W1[0:CH, 7, 0:P]
        select_in = W1[0:2 * E, 0:2, :].rearrange("j a c -> j (a c)")
        WT = sb("WT", [P, 4, D])
        gwT = sb("gwT", [P, E])
        b1T = sb("b1T", [P, CH])
        b2s = sb("b2s", [2 * E, D])
        gbias = sb("gbias", [P, E])
        rank = sb("rank", [P, E])
        mx = sb("mx", [P, 2, NB, G])
        rec = sb("rec", [P, 2, NB, G, 2])
        stats = sb("stats", [P, NB, 6])
        mean_var = sb("mean_var", [P, NB, 2])
        var_eps = sb("var_eps", [P, NB])
        rstd = sb("rstd", [P, NB])
        minus_half = sb("minus_half", [P, NB])
        gs = sb("gs", [P, 8, TB])
        gt = sb("gt", [P, 5, TB, E])
        w_tok = sb("w_tok", [P, NB, 2, E])
        wT = sb("wT", [2 * E, 2, S], FP32R)
        m_row = wT[0:G, :, :]

        ST = [pb(f"ST{i}") for i in range(3)]
        SM = [pb(f"SM{i}") for i in range(2)]
        OP = [pb(f"OP{i}") for i in range(2)]
        SIDE = pb("SIDE")
        HB = ST + [OP[1]]
        OE = SM
        WB = OP[0]

        scratch = nc.dram_tensor("scratch", [2, ROWS * H, S], FP32, kind="Internal").ap()

        const_in, mask_in, w1_in = sem("const_in"), sem("mask_in"), sem("w1_in")
        gb_in, va_zero = sem("gb_in"), sem("va_zero")
        x_loaded, xres_loaded = sem("x_loaded"), sem("xres_loaded")
        w2_in = [sem(f"w2_in{e}") for e in range(E)]
        cleared_dve, cleared_pool, idb_ready = sem("cleared_dve"), sem("cleared_pool"), sem("idb_ready")
        side_filled, side_drained = sem("side_filled"), sem("side_drained")
        hi_ready, scratch_in, stack_in, mrow_in = sem("hi_ready"), sem("scratch_in"), sem("stack_in"), sem("mrow_in")
        smax_filled, smax_read = sem("smax_filled"), sem("smax_read")
        st_filled, exp_done, masked, pv_done, o_copied = sem("st_filled"), sem("exp_done"), sem("masked"), sem("pv_done"), sem("o_copied")
        norm_step, ln_step, y_ready = sem("norm_step"), sem("ln_step"), sem("y_ready")
        gate_step, gexp_ready, gdiff_ready, kept = sem("gate_step"), sem("gexp_ready"), sem("gdiff_ready"), sem("kept")
        w1_split, w2_split, y_split = sem("w1_split"), sem("w2_split"), sem("y_split")
        h_filled, gelu_done, hhi_done, hlo_done = sem("h_filled"), sem("gelu_done"), sem("hhi_done"), sem("hlo_done")
        w2_done, wb_filled, wb_copied = sem("w2_done"), sem("wb_filled"), sem("wb_copied")
        scaled, added, ff_filled, ff_drained = sem("scaled"), sem("added"), sem("ff_filled"), sem("ff_drained")
        wtok_ready, ff_step, out_in = sem("wtok_ready"), sem("ff_step"), sem("out_in")
        sel_in, sel_ready = sem("sel_in"), sem("sel_ready")
        past_wait = sem("past_wait")
        var_ready, rstd_ready = sem("var_ready"), sem("rstd_ready")

        prf = PR[:, :, :, :].rearrange("p a g c -> p (a g c)")
        hf = [prf[:, S * i:S * (i + 1)] for i in range(4)]
        wb_sb = [prf[:, S * (4 + i):S * (5 + i)] for i in range(2)]
        part = [prf[:, S * (6 + i):S * (7 + i)] for i in range(2)]
        acc = [prf[:, S * (8 + i):S * (9 + i)] for i in range(2)]
        out_sb = [prf[:, S * (10 + i):S * (11 + i)] for i in range(2)]
        W2 = [W1[:, e, :].rearrange("p (c d) -> p c d", c=NCH) for e in range(E)]

        block = ctx.enter_context(nc.Block())

        x_v = x.rearrange("b (k p) d -> b p k d", p=P)
        out_v = out.rearrange("b (k p) d -> b p k d", p=P)
        STACK_IN = 16 * 2 * G
        SCRATCH_IN = 16 * 6

        def at_batch(v, b):
            return v[b] if isinstance(b, int) else v[bass.ds(b, 1)].rearrange("o p k d -> (o p) k d")

        def batches(eng, body):
            body(0, 0)
            with eng.Fori(0, (B - 2) // 2) as i:
                body(i * 2 + 1, 1)
                body(i * 2 + 2, 0)
            body(B - 1, 1)

        def own_wait(eng):
            eng.sem_inc(past_wait, 1)

        def unit_of(b, p, s):
            return (b, p, s) if s < UNITS else (b + 1, 1 - p, s - UNITS)

        @block.sync
        def _(sp):
            sp.dma_start(idf[:], ident[:, :]).then_inc(const_in, 16)
            sp.dma_start(x_in[:], x_v[0]).then_inc(x_loaded, 16)
            for i in range(3):
                sp.dma_start(wrows[:, i, :], qkv[i * D:(i + 1) * D, :]).then_inc(const_in, 16)
            sp.dma_start(wrows[:, 3, :], wo[:, :]).then_inc(const_in, 16)
            sp.dma_start(gate_rows, gate_w[:, :]).then_inc(gb_in, 16)
            sp.dma_start(b1_rows, b1.rearrange("e (c p) -> (e c) p", p=P)).then_inc(gb_in, 16)
            sp.dma_start(mask_q[:], maskq[:, :]).then_inc(mask_in, 16)
            sp.dma_start(mask_k[:], maskk[:, :]).then_inc(mask_in, 16)
            sp.dma_start(b2s[0:E, :], b2[:, :]).then_inc(mask_in, 16)
            sp.dma_start(b2s[E:2 * E, :], b2[:, :]).then_inc(mask_in, 16)
            sp.dma_start(gbias[:], gate_b.rearrange("(o e) -> o e", o=1).broadcast_to([P, E])).then_inc(mask_in, 16)
            sp.dma_start(select_in, select[:, :]).then_inc(sel_in, 16)
            sp.dma_start(y[:], x_v[0]).then_inc(xres_loaded, 16)

            def m_rows(b, p, s):
                sp.wait_ge(side_drained, side_of(f"m{s}", b))
                for g in range(G):
                    sp.dma_start(QS[32 * g + ROW_M:32 * g + ROW_M + 1, p, G * g + s, :].bitcast(FP32),
                                 m_row[g:g + 1, s % 2, :].bitcast(FP32)).then_inc(mrow_in, 16)

            def stacks(b, p):
                for j, name in enumerate("qk"):
                    sp.wait_ge(side_drained, side_of(name, b))
                    for t, lo in enumerate([(0, 0, 1), (0, 1, 0)][j]):
                        sp.dma_start(scratch[j, P * t:P * (t + 1)],
                                     split[:, 2 * j + lo, :].bitcast(FP32)).then_inc(scratch_in, 16)
                sp.wait_ge(scratch_in, (b + 1) * SCRATCH_IN + 32)
                if is_at(b, 0):
                    sp.wait_ge(cleared_dve, 1)
                for j in range(2):
                    for g in range(G):
                        rows = slice(32 * g, 32 * g + ROWS)
                        dst = KS[rows, p, :, :] if j else QS[rows, p, 4 * g:4 * g + 4, :]
                        src = scratch[j].rearrange("(r h) c -> r h c", h=H)[:, 4 * g:4 * g + 4, :]
                        sp.dma_start(dst.bitcast(FP32), src).then_inc(stack_in, 16)

            for j in range(2):
                sp.dma_start(scratch[j, 3 * P:ROWS * H], stack_rows[j]).then_inc(scratch_in, 16)
            stacks(0, 0)
            sp.wait_ge(cleared_pool, 1)
            sp.wait_ge(side_filled, side_of("xT", 0))
            sp.dma_start(x_in[:], x_v[1]).then_inc(x_loaded, 16)
            m_rows(0, 0, 0)
            sp.wait_ge(sel_ready, 1)
            sp.dma_start(W1[:], w1.rearrange("e d f -> d e f")).then_inc(w1_in, 16)

            def body(b, p):
                m_rows(b, p, 1)
                if not is_at(b, B - 1):
                    if not is_at(b, 0):
                        sp.wait_ge(st_filled, b * (SLOTS * NC3))
                        own_wait(nc.sync)
                        sp.wait_ge(stack_in, (b + 1) * STACK_IN)
                        own_wait(nc.sync)
                    else:
                        sp.wait_ge(stack_in, STACK_IN)
                    stacks(b + 1, 1 - p)
                m_rows(b, p, 2)
                m_rows(b, p, 3)
                if is_at(b, B - 1):
                    for e in range(E):
                        sp.wait_ge(w1_split, 2 * (e + 1))
                        sp.dma_start(W2[e], w2[e].rearrange("(c p) d -> p c d", p=P)).then_inc(w2_in[e], 16)
                if not is_at(b, B - 1):
                    sp.wait_ge(side_filled, side_of("xT", b + 1))
                    own_wait(nc.sync)
                    sp.dma_start(x_in[:], at_batch(x_v, (b + 2) % B)).then_inc(x_loaded, 16)
                    m_rows(b + 1, 1 - p, 0)
                if not is_at(b, 0):
                    sp.wait_ge(side_filled, side_of("yT", b - 1))
                    sp.dma_start(y[:], at_batch(x_v, b)).then_inc(xres_loaded, 16)

            batches(sp, body)
            def store(f, p):
                sp.wait_ge(ff_drained, ff_side_of("out", f))
                sp.dma_start(at_batch(out_v, f), out_sb[p].rearrange("p (k d) -> p k d", k=NB)).then_inc(out_in, 16)

            batches(sp, store)
            sp.wait_ge(out_in, 16 * (B + 1))
            sp.wait_ge(x_loaded, 16 * (B + 1))
            sp.wait_ge(scratch_in, B * SCRATCH_IN + 32)

        @block.gpsimd
        def _(pool):
            nc.gpsimd.sem_inc(kept, 1)
            nc.gpsimd.sem_inc(out_in, 16)
            nc.gpsimd.memset(KS[:, 1].bitcast(FP32), 0.0)
            nc.gpsimd.memset(VA[:], 0.0).then_inc(va_zero, 1)
            pool.wait_ge(va_zero, 1)
            for p in range(2):
                for t in range(2):
                    nc.gpsimd.memset(VA[:, p, :, t::2, VW * t + DH:VW * (t + 1)], 1.0)
            nc.gpsimd.memset(minus_half[:], -0.5)
            nc.gpsimd.memset(QS[:, 1].bitcast(FP32), 0.0).then_inc(cleared_pool, 1)

            pool.wait_ge(sel_in, 16)
            nc.gpsimd.tensor_copy(sel[:].rearrange("j e p -> j (e p)"), select_in).then_inc(sel_ready, 1)

            def mask_own(b, s):
                pool.wait_ge(exp_done, (b * UNITS + s + 1) * (G * NC3))
                own_wait(nc.gpsimd)
                for kb in range(NB):
                    own = PR[:, s % 2, :, OFF[kb]:OFF[kb] + P]
                    nc.gpsimd.affine_select(own, own, pattern=[[0, G], [1, P]], compare_op=ALU.is_ge, fill=0.0,
                                            base=0, channel_multiplier=-1).then_inc(masked, 1)

            def power(count):
                pool.wait_ge(var_ready, count + 1)
                nc.gpsimd.tensor_tensor(rstd[:], var_eps[:], minus_half[:], ALU.pow).then_inc(rstd_ready, 1)

            def normalise(f):
                power(f)
                pool.wait_ge(rstd_ready, f + 1)
                own_wait(nc.gpsimd)
                for k in range(NB):
                    last = nc.gpsimd.tensor_scalar(y[:, k, :], y[:, k, :], mean_var[:, k, 0:1], rstd[:, k:k + 1],
                                                   ALU.subtract, ALU.mult)
                last.then_inc(y_ready, 1)

            def keep(f):
                pool.wait_ge(side_drained, side_of("yT", f))
                nc.gpsimd.tensor_copy(yT_all[:, bass.ds(f, 1), :].rearrange("p o c -> p (o c)"), T[:, :]).then_inc(kept, 1)

            def body(b, p):
                mask_own(b, 0)
                mask_own(b, 1)
                if not is_at(b, 0):
                    normalise(b - 1)
                mask_own(b, 2)
                if not is_at(b, 0):
                    keep(b - 1)
                mask_own(b, 3)

            batches(pool, body)

            def add(f, p, e):
                pool.wait_ge(scaled, f * E + e + 1)
                if e == 0:
                    pool.wait_ge(ff_drained, ff_side_of("b2", f))
                else:
                    pool.wait_ge(added, f * E + e)
                nc.gpsimd.tensor_tensor(acc[p], acc[p], part[e % 2], ALU.add).then_inc(added, 1)

            def ff_body(f, p):
                for e in range(E):
                    add(f, p, e)
                    if is_at(f, 0) and e == 0:
                        normalise(B - 1)
                    if is_at(f, 0) and e == 2:
                        keep(B - 1)
                    if e == 1 and not is_at(f, 0):
                        power(f - 1 + B)

            batches(pool, ff_body)
            power(B - 1 + B)

        @block.scalar
        def _(act):
            def copy_side(dst, src, name, b, scale=None):
                act.wait_ge(side_filled, side_of(name, b))
                if scale is None:
                    return nc.scalar.copy(dst, src)
                return nc.scalar.mul(dst, src, scale)

            def evacuate(name, b, p):
                if name == "xT":
                    copy_side(xT[:], SIDE[:], name, b).then_inc(side_drained, 1)
                elif name in "qk":
                    if not is_at(b, 0):
                        act.wait_ge(scratch_in, b * SCRATCH_IN + 32)
                    copy_side(split[:, 2 * "qk".index(name), :], SIDE[:], name, b).then_inc(hi_ready, 1)
                elif name == "V":
                    if is_at(b, 0):
                        act.wait_ge(cleared_pool, 1)
                    elif not is_at(b, 1):
                        act.wait_ge(pv_done, (b - 1) * UNITS)
                    src = SIDE[:].rearrange("p (k h t d) -> p k h t d", k=NB, t=2, d=DH)
                    for t in range(2):
                        last = copy_side(VA[:, p, :, t::2, VW * t:VW * t + DH], src[:, :, :, t, :], name, b)
                    last.then_inc(side_drained, 1)
                elif name == "gb":
                    copy_side(gwT[:], SIDE[:, 0:E], name, b)
                    copy_side(b1T[:], SIDE[:, E:E + CH], name, b).then_inc(side_drained, 1)
                elif name[0] == "m":
                    s = int(name[1])
                    u = b * UNITS + s
                    if not (isinstance(u, int) and u < 2):
                        act.wait_ge(mrow_in, (u - 1) * (16 * G))
                    copy_side(m_row[:, s % 2, :], SIDE[0:G, :], name, b, -1.0).then_inc(side_drained, 1)
                elif name == "AT":
                    if not is_at(b, 0):
                        act.wait_ge(kept, b + 1)
                    copy_side(T[:], SIDE[:], name, b).then_inc(side_drained, 1)
                elif name == "yT":
                    copy_side(T[:], SIDE[:], name, b).then_inc(side_drained, 1)

            def gate_exp(late):
                blocks = slice(*GATES[late])
                act.wait_ge(gdiff_ready, late + 1)
                nc.scalar.activation(gs[:, 5, blocks], gs[:, 4, blocks], ACT.Exp).then_inc(gexp_ready, 1)

            def copy_o(b, half):
                act.wait_ge(pv_done, b * UNITS + 2 * half + 2)
                if not is_at(b, 0):
                    act.wait_ge(side_filled, side_of("OA" if half == 0 else "OB", b - 1))
                nc.scalar.copy(O_sb[:, half, :], OP[half][:]).then_inc(o_copied, 1)

            act.wait_ge(side_filled, 1)
            nc.scalar.copy(WT[:, 0:2, :].rearrange("p i (d h) -> p i d h", h=H),
                           SIDE[:, 0:2 * D].rearrange("p (i h d) -> p i d h", i=2, h=H))
            nc.scalar.copy(WT[:, 2:4, :], SIDE[:, 2 * D:4 * D].rearrange("p (i d) -> p i d", i=2)).then_inc(side_drained, 1)
            for name in START[1:]:
                evacuate(name, 0, 0)

            def body(b, p):
                for i in range(SLOTS):
                    s, g = divmod(i, G)
                    u = b * UNITS + s
                    if g == 0 and not (isinstance(u, int) and u < 2):
                        act.wait_ge(pv_done, u - 1)
                    for c in range(NC3):
                        act.wait_ge(st_filled, b * (SLOTS * NC3) + i * NC3 + c + 1)
                        n = CHUNK_AT[c + 1] - CHUNK_AT[c]
                        nc.scalar.activation(PR[:, s % 2, g, CHUNK_AT[c]:CHUNK_AT[c + 1]], ST[c][:, 0:n],
                                             ACT.Exp, scale=SCALE).then_inc(exp_done, 1)
                        for name in [n for j, n in body_steps(b) if j == place(i, c)]:
                            if name in ("xT", "q", "k", "V", "m0"):
                                evacuate(name, b + 1, 1 - p)
                            elif name[0] == "m":
                                evacuate(name, b, p)
                            else:
                                evacuate(name, b - 1, 1 - p)
                    if i == 4 and not is_at(b, 0):
                        copy_o(b - 1, 1)
                    if i == 12:
                        copy_o(b, 0)
                    if i == GATE_EXP_SLOT and is_at(b, B - 1):
                        gate_exp(0)

            batches(act, body)

            def copy_wT(f, p):
                act.wait_ge(ff_filled, ff_side_of("wT", f))
                nc.scalar.copy(wT[:, p, :], SIDE[0:2 * E, :]).then_inc(ff_drained, 1)

            def hidden_hi(f, m):
                n = f * CH + m
                act.wait_ge(gelu_done, n + 1)
                if not (isinstance(n, int) and n < 4):
                    act.wait_ge(w2_done, n - 3)
                nc.scalar.copy(KS[:, 0, m % 4, :], hf[m % 4]).then_inc(hhi_done, 1)

            def ff_body(f, p):
                for m in range(CH):
                    n = f * CH + m
                    act.wait_ge(h_filled, n + 1)
                    if not (isinstance(n, int) and n < 4):
                        act.wait_ge(hlo_done, n - 3)
                    nc.scalar.activation(hf[m % 4], HB[m % 4][:], ACT.Gelu, bias=b1T[:, m:m + 1]).then_inc(gelu_done, 1)
                    if m >= 1:
                        hidden_hi(f, m - 1)
                    elif not is_at(f, 0):
                        hidden_hi(f - 1, CH - 1)
                    if m % NCH == 1:
                        e = m // NCH
                        act.wait_ge(wb_filled, f * E + e + 1)
                        if not (is_at(f, 0) and e < 2):
                            act.wait_ge(scaled, f * E + e - 1)
                        nc.scalar.copy(wb_sb[e % 2], WB[:]).then_inc(wb_copied, 1)
                    if is_at(f, 0):
                        for name in [n for j, n in FF_TAIL if j == m and n in ("AT", "yT")]:
                            evacuate(name, B - 1, 1)
                        if m == GATE_EXP_AT:
                            gate_exp(1)
                    if m == 21 and not is_at(f, B - 1):
                        copy_wT(f + 1, 1 - p)

            act.wait_ge(mrow_in, B * UNITS * (16 * G))
            copy_wT(0, 0)
            copy_o(B - 1, 1)
            batches(act, ff_body)
            hidden_hi(B - 1, CH - 1)

        @block.vector
        def _(dve):
            for e in range(E):
                nc.vector.memset(rank[:, e:e + 1], float(E - e))
            nc.vector.memset(KS[:, 0].bitcast(FP32), 0.0)
            nc.vector.memset(OP[0][:], 0.0)
            nc.vector.memset(OP[1][:], 0.0)
            nc.vector.memset(QS[:, 0, 0:8].bitcast(FP32), 0.0)
            dve.wait_ge(const_in, 16 * 5)
            nc.vector.tensor_copy(idb[:], idf[:]).then_inc(idb_ready, 1)

            def chain(sem_, before, per):
                k = [0]

                def step(ins):
                    k[0] += 1
                    ins.then_inc(sem_, 1)
                    dve.wait_ge(sem_, before + k[0])
                    assert k[0] <= per
                return step

            def low_part(name, b):
                j = "qk".index(name)
                dve.wait_ge(hi_ready, b * 2 + j + 1)
                nc.vector.tensor_tensor(split[:, 2 * j + 1, :], SIDE[:], split[:, 2 * j, :].bitcast(FP32),
                                        ALU.subtract).then_inc(side_drained, 1)

            def maxima(b, p, s, g, c):
                u = b * UNITS + s
                if g + c == 0 and not (isinstance(u, int) and u < 2):
                    s2 = (s + 2) % UNITS
                    dve.wait_ge(side_filled, side_of(f"m{s2}", b if s >= 2 else b - 1))
                n = b * (SLOTS * NC3) + (G * s + g) * NC3 + c
                dve.wait_ge(smax_filled, n + 1)
                own_wait(nc.vector)
                for qb, col in QUERY_CHUNKS[c]:
                    w = (qb + 1) * P
                    sm = SM[(g + c) % 2][:, col:col + w]
                    last = nc.vector.tensor_tensor_reduce(
                        out=sm, in0=sm, in1=mask_q[:, S - w:S], scale=1.0,
                        scalar=BELOW, op0=ALU.add, op1=ALU.max, accum_out=mx[:, s % 2, qb, g:g + 1])
                last.then_inc(smax_read, 1)

            def bn_stats(src, step):
                for k in range(NB):
                    last = nc.vector.bn_stats(stats[:, k, :], src[:, k, :])
                step(last)

            def variance(step):
                own_wait(nc.vector)
                for k in range(NB):
                    last = nc.vector.bn_aggr(mean_var[:, k, :], stats[:, k, :])
                step(last)
                nc.vector.tensor_scalar_add(var_eps[:], mean_var[:, :, 1], EPS).then_inc(var_ready, 1)

            def moments(b, part):
                step = chain(ln_step, b * 2 + part, 1)
                if part == 0:
                    dve.wait_ge(side_drained, side_of("proj", b))
                    own_wait(nc.vector)
                    bn_stats(y, step)
                else:
                    variance(step)

            def post(name, b):
                dve.wait_ge(side_filled, side_of(name, b))
                if name in ("OA", "OB"):
                    half = "OA OB".split().index(name)
                    step = chain(norm_step, b * 2 + half, 1)
                    o = SIDE[:].rearrange("p (k g w) -> p k g w", k=NB, g=G)
                    step(nc.vector.reciprocal(rec[:, half], o[:, :, :, DH:2 * VW:VW]))
                    a = att[:].rearrange("p k (g s d) -> p k g s d", g=G, s=UNITS)
                    for t in range(2):
                        last = nc.vector.tensor_tensor(
                            a[:, :, :, 2 * half + t, :], o[:, :, :, VW * t:VW * t + DH],
                            rec[:, half, :, :, t].unsqueeze(3).broadcast_to([P, NB, G, DH]), ALU.mult)
                    last.then_inc(side_drained, 1)
                elif name == "proj":
                    dve.wait_ge(xres_loaded, (b + 1) * 16)
                    last = nc.vector.tensor_tensor(y[:], SIDE[:].rearrange("p (k d) -> p k d", k=NB), y[:], ALU.add)
                    last.then_inc(side_drained, 1)
                elif name == "gate":
                    nc.vector.tensor_tensor(
                        logits[:, bass.ds(b * NB, NB), :], SIDE[:, 0:NB * E].rearrange("p (k e) -> p k e", k=NB),
                        gbias[:, :].unsqueeze(1).broadcast_to([P, NB, E]), ALU.add).then_inc(side_drained, 1)

            def gate(late, stage):
                lo_, hi_ = GATES[late]
                n = hi_ - lo_
                step = chain(gate_step, late * sum(GATE_STEPS) + sum(GATE_STEPS[:stage]), GATE_STEPS[stage])
                V = nc.vector
                logit, w = logits[:, lo_:hi_], w_all[:, lo_:hi_]
                best, best_rank, second, second_rank, diff, ex, a, b_ = [gs[:, i, lo_:hi_] for i in range(8)]
                t = [gt[:, i, lo_:hi_] for i in range(5)]
                wide = lambda x_: x_.unsqueeze(2).broadcast_to([P, n, E])
                ranks = rank[:, :].unsqueeze(1).broadcast_to([P, n, E])
                if stage == 0:
                    dve.wait_ge(side_drained, side_of("gate", B - 1 if late else B - 3))
                    step(V.tensor_reduce(best, logit, AX.X, ALU.max))
                    step(V.tensor_tensor(t[0], logit, wide(best), ALU.is_equal))
                    step(V.tensor_tensor(t[1], t[0], ranks, ALU.mult))
                    step(V.tensor_reduce(best_rank, t[1], AX.X, ALU.max))
                    step(V.tensor_tensor(t[2], t[1], wide(best_rank), ALU.is_equal))
                if stage == 1:
                    step(V.tensor_scalar_mul(t[1], t[2], BELOW))
                    step(V.tensor_tensor(t[0], t[1], logit, ALU.add))
                    step(V.tensor_reduce(second, t[0], AX.X, ALU.max))
                    V.tensor_tensor(diff, second, best, ALU.subtract).then_inc(gdiff_ready, 1)
                if stage == 2:
                    step(V.tensor_tensor(t[1], t[0], wide(second), ALU.is_equal))
                    step(V.tensor_tensor(t[3], t[1], ranks, ALU.mult))
                    step(V.tensor_reduce(second_rank, t[3], AX.X, ALU.max))
                    step(V.tensor_tensor(t[4], t[3], wide(second_rank), ALU.is_equal))
                if stage == 3:
                    dve.wait_ge(gexp_ready, late + 1)
                    step(V.tensor_scalar_add(a, ex, 1.0))
                    step(V.reciprocal(b_, a))
                    step(V.tensor_tensor(a, ex, b_, ALU.mult))
                    step(V.tensor_tensor(t[0], t[2], wide(b_), ALU.mult))
                    step(V.tensor_tensor(t[1], t[4], wide(a), ALU.mult))
                    step(V.tensor_tensor(t[3], t[0], t[1], ALU.add))
                    step(V.tensor_copy(w[:, :, 0, :], t[3]))
                    step(V.tensor_tensor(w[:, :, 1, :], t[3], w[:, :, 0, :].bitcast(FP32), ALU.subtract))

            def take_w(f):
                dve.wait_ge(kept, f + 2)
                nc.vector.tensor_copy(w_tok[:].rearrange("p k t e -> p (k t e)"),
                                      w_all[:, bass.ds(f * NB, NB)].bitcast(FP32).rearrange("p k t e -> p (k t e)")).then_inc(wtok_ready, 1)

            def yT_of(f):
                return yT_all[:, bass.ds(f, 1), :].rearrange("p o c -> p (o c)")

            def split_y(f, p, lo):
                if lo:
                    dve.wait_ge(y_split, f * 2 + 1)
                    nc.vector.tensor_tensor(split[:, 2 * p + 1, :], yT_of(f), split[:, 2 * p, :].bitcast(FP32),
                                            ALU.subtract).then_inc(y_split, 1)
                else:
                    nc.vector.tensor_copy(split[:, 2 * p, :], yT_of(f)).then_inc(y_split, 1)

            def split_weights(j, e):
                done = (w1_split, w2_split)[j]
                w = W1[:, e, :]
                nc.vector.tensor_copy(QS[:, j, 2 * e, :], w).then_inc(done, 1)
                dve.wait_ge(done, 2 * e + 1)
                nc.vector.tensor_tensor(QS[:, j, 2 * e + 1, :], w, QS[:, j, 2 * e, :].bitcast(FP32),
                                        ALU.subtract).then_inc(done, 1)

            def split_w1(e):
                dve.wait_ge(w1_in, 16)
                dve.wait_ge(st_filled, (B - 1) * (SLOTS * NC3))
                split_weights(0, e)

            def split_w2(e):
                dve.wait_ge(w2_in[e], 16)
                dve.wait_ge(st_filled, B * (SLOTS * NC3))
                split_weights(1, e)

            def prepare_experts(i):
                if W1_AT <= i < W1_AT + E // 2:
                    for e in range(2):
                        split_w1(2 * (i - W1_AT) + e)
                for stage in range(4):
                    if GATE_SLOTS[stage] == i:
                        gate(0, stage)
                if i == SLOTS - 1:
                    take_w(0)
                    dve.wait_ge(scratch_in, B * SCRATCH_IN + 32)
                    split_y(0, 0, 0)
                    split_y(0, 0, 1)

            low_part("q", 0)
            nc.vector.memset(QS[:, 0, 8:12].bitcast(FP32), 0.0)
            low_part("k", 0)
            nc.vector.memset(QS[:, 0, 12:16].bitcast(FP32), 0.0).then_inc(cleared_dve, 1)
            dve.wait_ge(mask_in, 16 * 5)
            for s in range(2):
                for g in range(G):
                    for c in range(NC3):
                        maxima(0, 0, s, g, c)

            def body(b, p):
                for i in range(SLOTS):
                    s, g = divmod(i, G)
                    for c in range(NC3):
                        if not (is_at(b, B - 1) and s >= 2):
                            maxima(*unit_of(b, p, s + 2), g, c)
                        for name in [n for j, n in body_steps(b) if j == place(i, c)]:
                            if name in ("q", "k"):
                                low_part(name, b + 1)
                            elif name in ("OA", "OB", "proj", "gate"):
                                post(name, b - 1)
                        if place(i, c) in MOMENTS_AT and not is_at(b, 0):
                            moments(b - 1, MOMENTS_AT.index(place(i, c)))
                    if is_at(b, B - 1):
                        prepare_experts(i)

            batches(dve, body)

            def start_sum(f, p):
                dve.wait_ge(ff_filled, ff_side_of("b2", f))
                nc.vector.tensor_tensor(acc[p], SIDE[:], yT_of(f), ALU.add).then_inc(ff_drained, 1)

            def weigh(f, e):
                dve.wait_ge(w2_done, f * CH + (e + 1) * NCH)
                dve.wait_ge(wb_copied, f * E + e + 1)
                if not (is_at(f, 0) and e < 2):
                    dve.wait_ge(added, f * E + e - 1)
                nc.vector.tensor_tensor(part[e % 2], OE[e % 2][:], wb_sb[e % 2], ALU.mult).then_inc(scaled, 1)

            def finish(f, p, steps):
                result = SIDE[:].rearrange("p (k d) -> p k d", k=NB)
                dst = out_sb[p].rearrange("p (k d) -> p k d", k=NB)
                step = chain(ff_step, f * 2 + min(steps), 2)
                if 0 in steps:
                    dve.wait_ge(ff_filled, ff_side_of("out", f))
                    bn_stats(result, step)
                if 1 in steps:
                    variance(step)
                if 2 in steps:
                    dve.wait_ge(rstd_ready, f + B + 1)
                    dve.wait_ge(out_in, (f + 1) * 16)
                for k in range(NB):
                    if 2 + k // 2 in steps:
                        last = nc.vector.tensor_scalar(dst[:, k, :], result[:, k, :], mean_var[:, k, 0:1],
                                                       rstd[:, k:k + 1], ALU.subtract, ALU.mult)
                if 3 in steps:
                    last.then_inc(ff_drained, 1)

            def ff_body(f, p):
                for m in range(CH):
                    n = f * CH + m
                    if is_at(f, 0) and m % NCH == 0 and m // NCH + 1 < E:
                        split_w2(m // NCH + 1)
                    dve.wait_ge(hhi_done, n + 1)
                    nc.vector.tensor_tensor(KS[:, 1, m % 4, :], hf[m % 4], KS[:, 0, m % 4, :].bitcast(FP32),
                                            ALU.subtract).then_inc(hlo_done, 1)
                    if m % NCH == 3:
                        e = m // NCH - 1
                        if e >= 0:
                            weigh(f, e)
                        elif not is_at(f, 0):
                            weigh(f - 1, E - 1)
                    if is_at(f, 0):
                        for name in [n for j, n in FF_TAIL if j == m and n in ("OA", "OB", "proj", "gate")]:
                            post(name, B - 1)
                        if m in FF_MOMENTS_AT:
                            moments(B - 1, FF_MOMENTS_AT.index(m))
                        for stage in range(4):
                            if GATE_AT[stage] == m:
                                gate(1, stage)
                    if m in FINISH_AT and not is_at(f, 0):
                        finish(f - 1, 1 - p, [FINISH_AT.index(m)])
                    if not is_at(f, B - 1):
                        if m == 14:
                            dve.wait_ge(ff_filled, ff_side_of("wT", f))
                            take_w(f + 1)
                        if m == 25:
                            start_sum(f + 1, 1 - p)
                        if m == 26:
                            split_y(f + 1, 1 - p, 0)
                        if m == 28:
                            split_y(f + 1, 1 - p, 1)

            dve.wait_ge(pv_done, B * UNITS - 1)
            start_sum(0, 0)
            split_w2(0)
            batches(dve, ff_body)
            weigh(B - 1, E - 1)
            finish(B - 1, 1, [0, 1, 2, 3])

        @block.tensor
        def _(pe):
            mm = nc.tensor.matmul

            def side(name, b):
                pe.wait_ge(side_drained, side_of(name, b) - 1)

            def blocks(k):
                return slice(k * P, (k + 1) * P)

            def side_step(name, b):
                side(name, b)
                if name == "xT":
                    pe.wait_ge(x_loaded, (b + 1) * 16)
                    for k in range(NB):
                        last = nc.tensor.transpose(SIDE[:, blocks(k)], x_in[:, k, :], idf[:])
                elif name in ("q", "k"):
                    last = mm(SIDE[:], WT[:, "qk".index(name), :], xT[:], start=True, stop=True)
                elif name == "V":
                    for k in range(NB):
                        last = mm(SIDE[:, blocks(k)], xT[:, blocks(k)], WT[:, 2, :], start=True, stop=True)
                elif name == "gb":
                    pe.wait_ge(gb_in, 16 * 2)
                    nc.tensor.transpose(SIDE[:, 0:E], gate_rows, idf[0:E, 0:E])
                    last = nc.tensor.transpose(SIDE[:, E:E + CH], b1_rows, idf[0:CH, 0:CH])
                elif name[0] == "m":
                    s = int(name[1])
                    pe.wait_ge(smax_read, (b * UNITS + s + 1) * (G * NC3))
                    for k in range(NB):
                        last = nc.tensor.transpose(SIDE[0:G, blocks(k)], mx[:, s % 2, k, :], idf[:])
                elif name in ("OA", "OB"):
                    half = "OA OB".split().index(name)
                    pe.wait_ge(o_copied, b * 2 + half + 1)
                    for k in range(NB):
                        last = nc.tensor.transpose(SIDE[:, blocks(k)], O_sb[:, half, blocks(k)], idf[:])
                elif name == "AT":
                    for k in range(NB):
                        last = nc.tensor.transpose(SIDE[:, blocks(k)], att[:, k, :], idf[:])
                elif name == "proj":
                    for k in range(NB):
                        last = mm(SIDE[:, blocks(k)], T[:, blocks(k)], WT[:, 3, :], start=True, stop=True)
                elif name == "yT":
                    pe.wait_ge(y_ready, b + 1)
                    for k in range(NB):
                        last = nc.tensor.transpose(SIDE[:, blocks(k)], y[:, k, :], idf[:])
                elif name == "gate":
                    for k in range(NB):
                        last = mm(SIDE[:, k * E:(k + 1) * E], T[:, blocks(k)], gwT[:], start=True, stop=True)
                last.then_inc(side_filled, 1)

            def scores_for_max(b, p, s, g, c):
                n = b * (SLOTS * NC3) + (G * s + g) * NC3 + c
                if not (isinstance(n, int) and n < 2):
                    pe.wait_ge(smax_read, n - 1)
                for qb, col in QUERY_CHUNKS[c]:
                    w = (qb + 1) * P
                    last = mm(SM[(g + c) % 2][:, col:col + w], QS[:, p, G * g + s, blocks(qb)], KS[:, p, s, 0:w],
                              start=True, stop=True)
                last.then_inc(smax_filled, 1)

            def scores(b, p, s, g, c):
                n = b * (SLOTS * NC3) + (G * s + g) * NC3 + c
                if not (isinstance(n, int) and n < 3):
                    pe.wait_ge(exp_done, n - 2)
                for kb, col in KEY_CHUNKS[c]:
                    w = S - kb * P
                    to = 2 * P if kb == 0 else w
                    last = mm(ST[c][:, col:col + w], KS[:, p, s, blocks(kb)], QS[:, p, G * g + s, kb * P:S],
                              start=True, stop=w == P, skip_group_check=True)
                    if to > P:
                        last = mm(ST[c][:, col + P:col + to], idb[:], mask_k[:, P:to], start=False, stop=True,
                                  skip_group_check=True)
                last.then_inc(st_filled, 1)

            def outputs(b, p, s, kb):
                pe.wait_ge(masked, (b * UNITS + s) * NB + kb + 1)
                if kb == 0:
                    if s == 0:
                        pe.wait_ge(side_drained, side_of("V", b))
                    if s % 2 == 0 and not is_at(b, 0):
                        pe.wait_ge(o_copied, b * 2 - 1 + s // 2)
                for g in range(G):
                    last = mm(OP[s // 2][32 * g:32 * g + 2 * VW, kb * P:S], VA[:, p, kb, G * g + s, :],
                              PR[:, s % 2, g, OFF[kb]:OFF[kb] + S - kb * P],
                              start=(s % 2 == 0 and kb == 0), stop=(s % 2 == 1 and kb == NB - 1), skip_group_check=True)
                if kb == NB - 1:
                    last.then_inc(pv_done, 1)

            def side_steps_of(b, where):
                for name in [n for j, n in body_steps(b) if j == where]:
                    if name in ("xT", "q", "k", "V", "m0"):
                        side_step(name, b + 1)
                    elif name[0] == "m":
                        side_step(name, b)
                    else:
                        side_step(name, b - 1)

            pe.wait_ge(const_in, 16 * 5)
            for i in range(4):
                last = nc.tensor.transpose(SIDE[:, blocks(i)], wrows[:, i, :], idf[:])
            last.then_inc(side_filled, 1)
            for name in START[1:6]:
                side_step(name, 0)
            pe.wait_ge(stack_in, STACK_IN)
            for s in range(2):
                for g in range(G):
                    for c in range(NC3):
                        scores_for_max(0, 0, s, g, c)
                if s == 0:
                    side_step("m0", 0)
            pe.wait_ge(mask_in, 16 * 5)
            pe.wait_ge(idb_ready, 1)
            pe.wait_ge(cleared_dve, 1)

            def body(b, p):
                for i in range(SLOTS):
                    s, g = divmod(i, G)
                    if g == 0:
                        pe.wait_ge(mrow_in, (b * UNITS + s + 1) * (16 * G))
                    if i == 8 and not is_at(b, B - 1):
                        pe.wait_ge(stack_in, (b + 2) * STACK_IN)
                    for c in range(NC3):
                        scores(b, p, s, g, c)
                        if not (is_at(b, B - 1) and s >= 2):
                            scores_for_max(*unit_of(b, p, s + 2), g, c)
                        side_steps_of(b, place(i, c))
                    if s:
                        outputs(b, p, s - 1, g)
                    elif not is_at(b, 0):
                        outputs(b - 1, 1 - p, UNITS - 1, g)

            batches(pe, body)

            def weights_T(f, p):
                if is_at(f, 0):
                    pe.wait_ge(side_drained, BASE_TAIL)
                else:
                    pe.wait_ge(ff_drained, ff_side_of("wT", f) - 1)
                if is_at(f, 1):
                    pe.wait_ge(side_drained, side_of("gate", B - 1))
                pe.wait_ge(wtok_ready, f + 1)
                for k in range(NB):
                    last = nc.tensor.transpose(SIDE[0:2 * E, blocks(k)], w_tok[:, k].rearrange("p t e -> p (t e)"), idf[:])
                last.then_inc(ff_filled, 1)

            def biases(f, p):
                pe.wait_ge(ff_drained, ff_side_of("b2", f) - 1)
                mm(SIDE[:], b2s[:], wT[:, p, :].bitcast(FP32), start=True, stop=True).then_inc(ff_filled, 1)

            def result(f, p):
                pe.wait_ge(ff_drained, ff_side_of("out", f) - 1)
                pe.wait_ge(added, (f + 1) * E)
                for k in range(NB):
                    last = nc.tensor.transpose(SIDE[:, blocks(k)], acc[p][:, blocks(k)], idf[:])
                last.then_inc(ff_filled, 1)

            def spread(f, p, e):
                if not (is_at(f, 0) and e == 0):
                    pe.wait_ge(wb_copied, f * E + e)
                mm(WB[:], sel[:, e, :], wT[:, p, :], start=True, stop=True).then_inc(wb_filled, 1)

            def first_product(f, p, m):
                e, c = divmod(m, NCH)
                n = f * CH + m
                if m == 0:
                    pe.wait_ge(y_split, (f + 1) * 2)
                if is_at(f, 0) and m == 3:
                    pe.wait_ge(o_copied, B * 2)
                if is_at(f, 0) and c == 0:
                    pe.wait_ge(w1_split, 2 * (e + 1))
                if not (isinstance(n, int) and n < 4):
                    pe.wait_ge(gelu_done, n - 3)
                for k, (a, b_) in enumerate(((0, 0), (0, 1), (1, 0))):
                    last = mm(HB[m % 4][:], QS[:, 0, 2 * e + a, c * P:(c + 1) * P], split[:, 2 * p + b_, :],
                              start=(k == 0), stop=(k == 2))
                last.then_inc(h_filled, 1)

            def second_product(f, m):
                e, c = divmod(m, NCH)
                pe.wait_ge(hlo_done, f * CH + m + 1)
                if is_at(f, 0) and c == 0:
                    pe.wait_ge(w2_split, 2 * (e + 1))
                if c == 0 and not (is_at(f, 0) and e < 2):
                    pe.wait_ge(scaled, f * E + e - 1)
                for k, (a, b_) in enumerate(((0, 0), (0, 1), (1, 0))):
                    last = mm(OE[e % 2][:], QS[:, 1, 2 * e + a, c * P:(c + 1) * P], KS[:, b_, m % 4, :],
                              start=(c == 0 and k == 0), stop=(c == NCH - 1 and k == 2))
                last.then_inc(w2_done, 1)

            def ff_body(f, p):
                for m in range(CH):
                    if m % NCH == 0:
                        spread(f, p, m // NCH)
                    first_product(f, p, m)
                    if m >= LAG:
                        second_product(f, m - LAG)
                    elif not is_at(f, 0):
                        second_product(f - 1, CH + m - LAG)
                    if is_at(f, 0):
                        for name in [n for j, n in FF_TAIL if j == m]:
                            if name == FF_TAIL[0][1]:
                                pe.wait_ge(ff_drained, ff_side_of("b2", 0))
                            side_step(name, B - 1)
                    if m == 10 and not is_at(f, 0):
                        result(f - 1, 1 - p)
                    if not is_at(f, B - 1):
                        if m == 20:
                            weights_T(f + 1, 1 - p)
                        if m == 24:
                            biases(f + 1, 1 - p)

            weights_T(0, 0)
            biases(0, 0)
            for kb in range(NB):
                outputs(B - 1, 1, UNITS - 1, kb)
            pe.wait_ge(sel_ready, 1)
            pe.wait_ge(o_copied, B * 2 - 1)
            pe.wait_ge(exp_done, B * (SLOTS * NC3))
            pe.wait_ge(smax_read, B * (SLOTS * NC3))
            batches(pe, ff_body)
            for m in range(CH - LAG, CH):
                second_product(B - 1, m)
            result(B - 1, 1)




def kernel(**inputs):
    import numpy as np
    import concourse.bacc as bacc
    from concourse import mybir as my
    from concourse.bass_utils import run_bass_kernel_spmd

    import ml_dtypes
    i = np.arange(P)[:, None]
    j = np.arange(P)[None, :]

    def allowed(d):
        far = i + d * P - j
        return ((far >= 0) & (far < WINDOW)) | ((far >= WINDOW + DILATION) & (far % DILATION == 0))

    masks = [np.where(allowed(d), 0.0, MASKED).astype(ml_dtypes.bfloat16) for d in (0, 1, 2, 3)]
    maskq = np.concatenate(masks[::-1], axis=1)
    maskk = np.concatenate([np.ascontiguousarray(m.T) for m in masks], axis=1)
    token, residue = np.arange(S)[None, :], np.arange(FAR)[:, None]
    rows_q = np.where((token >= 2 * P) & (token % FAR != residue), MASKED, 0.0)
    rows_k = np.where((token < P) & (token % FAR == residue), 1.0, 0.0)
    stack_rows = np.stack([np.repeat(np.concatenate([np.full((1, S), one), rows]), H, axis=0)
                           for one, rows in ((0.0, rows_q), (1.0, rows_k))]).astype(np.float32)
    ident = np.eye(P, dtype=np.float32)
    select = np.repeat(np.tile(np.eye(E, dtype=np.float32), (2, 1)), P, axis=1)

    data = {k: np.ascontiguousarray(inputs[k]) for k in INPUTS}
    data.update(maskq=maskq, maskk=maskk, stack_rows=stack_rows, ident=ident, select=select)
    nc = bacc.Bacc("TRN2", target_bir_lowering=False, num_devices=1)
    aps = [nc.dram_tensor(f"in_{k}", v.shape, my.dt.from_np(v.dtype), kind="ExternalInput").ap() for k, v in data.items()]
    out = nc.dram_tensor("out", (B, S, D), FP32, kind="ExternalOutput").ap()
    build(nc, *aps, out)
    r = run_bass_kernel_spmd(nc, [{f"in_{k}": v for k, v in data.items()}], core_ids=[0])
    return r.results[0]["out"]


INPUTS = ["L0_attn_x", "L0_attn_qkv", "L0_attn_wo", "L0_ffn_gate_w", "L0_ffn_gate_b", "L0_ffn_w1", "L0_ffn_b1",
          "L0_ffn_w2", "L0_ffn_b2"]
```
